# Optimizing a Trainium2 kernel written in Bass

```python
import numpy as np
import jax
import jax.numpy as jnp

def _softmax(x, axis=-1):
    return jax.nn.softmax(x, axis=axis)

def _gelu(x):
    return jax.nn.gelu(x, approximate=True)

def _silu(x):
    return jax.nn.silu(x)

def _sigmoid(x):
    return jax.nn.sigmoid(x)

def _layernorm(x, axis=-1, eps=1e-05):
    m = jnp.mean(x, axis=axis, keepdims=True)
    v = jnp.var(x, axis=axis, keepdims=True)
    return (x - m) / jnp.sqrt(v + eps)

def _scatter_add(tgt, idx, src, axis=0):
    return tgt.at[idx].add(src)

def _segment_sum(src, seg, n):
    return jax.ops.segment_sum(src, seg, n)
kernel_name = 'mk_adj_preln_d4_adj_r2_eba01f'

def setup_inputs(seed: int=0):
    np.random.seed(seed)
    _w = jnp.asarray

    def _rec_inputs():
        import jax
        import jax.numpy as jnp
        _gk = jax.random.key(seed)
        x = -0.0002928 + 1 * jax.random.normal(jax.random.fold_in(_gk, 1), (2048, 512), jnp.float32)
        _a = jax.random.bernoulli(jax.random.fold_in(_gk, 2), 0.000976562, (2048, 2048))
        _a = jnp.logical_or(_a, jnp.swapaxes(_a, -1, -2))
        _a = jnp.logical_or(_a, jnp.eye(2048, dtype=bool))
        _af = _a.astype(jnp.float32)
        adj = _af
        return (x, adj)
    x, adj = _rec_inputs()

    def _L0_gnn_setup():
        import jax, jax.numpy as jnp
        import numpy as np
        N = 2048
        D_IN = 512
        H = 16
        DH = D_IN // H
        ALPHA = 0.2
        MASK_VAL = -65500.0
        key = jax.random.key(seed)
        ks = jax.random.split(key, 7)
        x = jax.random.normal(ks[0], (N, D_IN), dtype=jnp.float32)
        adj = jax.random.randint(ks[1], (N, N), 0, 2).astype(jnp.float32)
        s = 1.0 / np.sqrt(D_IN)
        W_seq = jax.random.normal(ks[2], (D_IN, D_IN), dtype=jnp.float32) * s
        a1 = jax.random.normal(ks[3], (DH,), dtype=jnp.float32) / np.sqrt(DH)
        a2 = jax.random.normal(ks[4], (DH,), dtype=jnp.float32) / np.sqrt(DH)
        W_out = jax.random.normal(ks[5], (D_IN, D_IN), dtype=jnp.float32) * s
        b_out = jax.random.normal(ks[6], (D_IN,), dtype=jnp.float32) * 0.01
        return {'x': x, 'adj': adj, 'W_seq': W_seq, 'a1': a1, 'a2': a2, 'W_out': W_out, 'b_out': b_out}
    _L0_gnn_all = _L0_gnn_setup()
    _L0_gnn_in = {k: v for k, v in _L0_gnn_all.items() if k in ('W_seq', 'a1', 'a2', 'W_out', 'b_out')}
    del _L0_gnn_all

    def _L1_gnn_setup():
        import jax, jax.numpy as jnp
        import numpy as np
        D_IN, D_ATTN, STEPS = (512, 64, 2)
        P_TOP, TAU, LN_EPS = (0.9, 1.0, 1e-05)
        N = 2048

        def _xavier(key, shape):
            fan_in, fan_out = (shape[0], shape[1])
            lim = jnp.sqrt(6.0 / (fan_in + fan_out))
            return jax.random.uniform(key, shape, jnp.float32, -lim, lim)

        def _adj_from_feats(Xa, W1, W2, W3):
            Q = Xa @ W1
            K = Xa @ W3
            logits = Q @ W2 @ K.T / TAU
            n = logits.shape[1]
            order = jnp.argsort(-logits, axis=1)
            vals = jnp.take_along_axis(logits, order, axis=1)
            probs = jax.nn.softmax(vals, axis=1)
            csum = jnp.cumsum(probs, axis=1)
            k_i = jnp.sum(csum < P_TOP, axis=1) + 1
            keep = jnp.arange(n)[None, :] < k_i[:, None]
            masked_sorted = jnp.where(keep, vals, -jnp.inf)
            rows = jnp.arange(n)[:, None]
            masked = jnp.full_like(logits, -jnp.inf).at[rows, order].set(masked_sorted)
            return jax.nn.softmax(masked, axis=1)
        key = jax.random.key(seed)
        ks = jax.random.split(key, 12)
        X = jax.random.normal(ks[0], (N, D_IN), jnp.float32)
        S = jax.random.uniform(ks[1], (N, N), jnp.float32)
        W1 = _xavier(ks[2], (D_IN, D_ATTN))
        W3 = _xavier(ks[3], (D_IN, D_ATTN))
        W2 = _xavier(ks[4], (D_ATTN, D_ATTN))
        U1_0 = _xavier(ks[5], (D_IN, D_IN))
        U1_1 = _xavier(ks[6], (D_IN, D_IN))
        U2_0 = _xavier(ks[7], (D_IN, D_IN))
        U2_1 = _xavier(ks[8], (D_IN, D_IN))
        gamma = jnp.ones((D_IN,), jnp.float32)
        beta = jnp.zeros((D_IN,), jnp.float32)
        return {'X': X, 'S': S, 'W1': W1, 'W2': W2, 'W3': W3, 'U1_0': U1_0, 'U1_1': U1_1, 'U2_0': U2_0, 'U2_1': U2_1, 'gamma': gamma, 'beta': beta}
    _L1_gnn_all = _L1_gnn_setup()
    _L1_gnn_in = {k: v for k, v in _L1_gnn_all.items() if k in ('W1', 'W2', 'W3', 'U1_0', 'U1_1', 'U2_0', 'U2_1', 'gamma', 'beta')}
    del _L1_gnn_all

    def _L2_gnn_setup():
        import jax, jax.numpy as jnp
        import numpy as np
        ALPHA = 0.2
        NEG = -9000000000000000.0
        N, NFEAT, NHID, NHEADS = (2048, 512, 64, 8)
        EMB = NHID * NHEADS
        key = jax.random.key(seed)
        ks = jax.random.split(key, 16)
        x = jax.random.normal(ks[0], (N, NFEAT), dtype=jnp.float32)
        adj = (jax.random.uniform(ks[1], (N, N)) < 0.01).astype(jnp.float32)
        adj = jnp.maximum(adj, jnp.eye(N, dtype=jnp.float32))
        s = 0.05
        W = jax.random.normal(ks[2], (NHEADS, NFEAT, NHID), dtype=jnp.float32) * s
        a1 = jax.random.normal(ks[3], (NHEADS, NHID), dtype=jnp.float32) * s
        a2 = jax.random.normal(ks[4], (NHEADS, NHID), dtype=jnp.float32) * s
        W1 = jax.random.normal(ks[5], (EMB // 2, EMB), dtype=jnp.float32) * s
        b1 = jnp.zeros((EMB // 2,), dtype=jnp.float32)
        W2 = jax.random.normal(ks[6], (NFEAT // 4, EMB // 2), dtype=jnp.float32) * s
        b2 = jnp.zeros((NFEAT // 4,), dtype=jnp.float32)
        W3 = jax.random.normal(ks[7], (NFEAT // 2, NFEAT // 4), dtype=jnp.float32) * s
        b3 = jnp.zeros((NFEAT // 2,), dtype=jnp.float32)
        W4 = jax.random.normal(ks[8], (NFEAT, NFEAT // 2), dtype=jnp.float32) * s
        b4 = jnp.zeros((NFEAT,), dtype=jnp.float32)
        return {'x': x, 'adj': adj, 'W': W, 'a1': a1, 'a2': a2, 'W1': W1, 'b1': b1, 'W2': W2, 'b2': b2, 'W3': W3, 'b3': b3, 'W4': W4, 'b4': b4}
    _L2_gnn_all = _L2_gnn_setup()
    _L2_gnn_in = {k: v for k, v in _L2_gnn_all.items() if k in ('W', 'a1', 'a2', 'W1', 'b1', 'W2', 'b2', 'W3', 'b3', 'W4', 'b4')}
    del _L2_gnn_all

    def _L3_gnn_setup():
        import jax, jax.numpy as jnp
        import numpy as np
        N, H, E, HEADS = (1500, 512, 10000, 8)
        DK = H // HEADS
        key = jax.random.key(seed)
        k1, k2, k3, k4 = jax.random.split(key, 4)
        inst_feature = jax.random.normal(k1, (N, H), dtype=jnp.float32)
        rel_pair_index = jax.random.randint(k2, (E, 2), 0, N, dtype=jnp.int64)
        agg = jnp.zeros((N, N), dtype=jnp.float32)
        agg = agg.at[rel_pair_index[:, 0], rel_pair_index[:, 1]].set(1.0)
        agg = agg.at[jnp.arange(N), jnp.arange(N)].set(1.0)
        std = float(np.sqrt(2.0 / (H + DK)))
        Wq = jax.random.normal(k3, (H, H), dtype=jnp.float32) * std
        Wk = jax.random.normal(k4, (H, H), dtype=jnp.float32) * std
        bq = jnp.zeros((H,), dtype=jnp.float32)
        bk = jnp.zeros((H,), dtype=jnp.float32)
        return {'inst_feature': inst_feature, 'aggregator_matrix': agg, 'rel_pair_index': rel_pair_index, 'Wq': Wq, 'bq': bq, 'Wk': Wk, 'bk': bk}
    _L3_gnn_all = _L3_gnn_setup()
    _L3_gnn_in = {k: v for k, v in _L3_gnn_all.items() if k in ('rel_pair_index', 'Wq', 'bq', 'Wk', 'bk')}
    del _L3_gnn_all
    return {'x': x, 'adj': adj, 'L0_gnn_W_seq': _L0_gnn_in['W_seq'], 'L0_gnn_a1': _L0_gnn_in['a1'], 'L0_gnn_a2': _L0_gnn_in['a2'], 'L0_gnn_W_out': _L0_gnn_in['W_out'], 'L0_gnn_b_out': _L0_gnn_in['b_out'], 'L1_gnn_W1': _L1_gnn_in['W1'], 'L1_gnn_W2': _L1_gnn_in['W2'], 'L1_gnn_W3': _L1_gnn_in['W3'], 'L1_gnn_U1_0': _L1_gnn_in['U1_0'], 'L1_gnn_U1_1': _L1_gnn_in['U1_1'], 'L1_gnn_U2_0': _L1_gnn_in['U2_0'], 'L1_gnn_U2_1': _L1_gnn_in['U2_1'], 'L1_gnn_gamma': _L1_gnn_in['gamma'], 'L1_gnn_beta': _L1_gnn_in['beta'], 'L2_gnn_W': _L2_gnn_in['W'], 'L2_gnn_a1': _L2_gnn_in['a1'], 'L2_gnn_a2': _L2_gnn_in['a2'], 'L2_gnn_W1': _L2_gnn_in['W1'], 'L2_gnn_b1': _L2_gnn_in['b1'], 'L2_gnn_W2': _L2_gnn_in['W2'], 'L2_gnn_b2': _L2_gnn_in['b2'], 'L2_gnn_W3': _L2_gnn_in['W3'], 'L2_gnn_b3': _L2_gnn_in['b3'], 'L2_gnn_W4': _L2_gnn_in['W4'], 'L2_gnn_b4': _L2_gnn_in['b4'], 'L3_gnn_rel_pair_index': _L3_gnn_in['rel_pair_index'], 'L3_gnn_Wq': _L3_gnn_in['Wq'], 'L3_gnn_bq': _L3_gnn_in['bq'], 'L3_gnn_Wk': _L3_gnn_in['Wk'], 'L3_gnn_bk': _L3_gnn_in['bk']}

def reference(x, adj, L0_gnn_W_seq, L0_gnn_a1, L0_gnn_a2, L0_gnn_W_out, L0_gnn_b_out, L1_gnn_W1, L1_gnn_W2, L1_gnn_W3, L1_gnn_U1_0, L1_gnn_U1_1, L1_gnn_U2_0, L1_gnn_U2_1, L1_gnn_gamma, L1_gnn_beta, L2_gnn_W, L2_gnn_a1, L2_gnn_a2, L2_gnn_W1, L2_gnn_b1, L2_gnn_W2, L2_gnn_b2, L2_gnn_W3, L2_gnn_b3, L2_gnn_W4, L2_gnn_b4, L3_gnn_rel_pair_index, L3_gnn_Wq, L3_gnn_bq, L3_gnn_Wk, L3_gnn_bk):
    import jax
    import jax.numpy as jnp

    def _L0_gnn_ref(x, adj, W_seq, a1, a2, W_out, b_out):
        import jax, jax.numpy as jnp
        import numpy as np
        N = 2048
        D_IN = 512
        H = 16
        DH = D_IN // H
        ALPHA = 0.2
        MASK_VAL = -65500.0
        seq = (x @ W_seq).reshape(N, H, DH)
        score1 = jnp.einsum('nhd,d->hn', seq, a1)
        score2 = jnp.einsum('nhd,d->hn', seq, a2)
        scores = score1[:, :, None] + score2[:, None, :]
        scores = jax.nn.leaky_relu(scores, negative_slope=ALPHA)
        scores = scores + (1.0 - adj)[None, :, :] * MASK_VAL
        attn = jax.nn.softmax(scores, axis=-1)
        hidden = jnp.einsum('hij,jhd->ihd', attn, seq).reshape(N, D_IN)
        hidden = hidden @ W_out + b_out
        return jax.nn.elu(hidden)

    def _L1_gnn_ref(X, S, W1, W2, W3, U1_0, U1_1, U2_0, U2_1, gamma, beta):
        import jax, jax.numpy as jnp
        import numpy as np
        D_IN, D_ATTN, STEPS = (512, 64, 2)
        P_TOP, TAU, LN_EPS = (0.9, 1.0, 1e-05)
        N = 2048

        def _xavier(key, shape):
            fan_in, fan_out = (shape[0], shape[1])
            lim = jnp.sqrt(6.0 / (fan_in + fan_out))
            return jax.random.uniform(key, shape, jnp.float32, -lim, lim)

        def _adj_from_feats(Xa, W1, W2, W3):
            Q = Xa @ W1
            K = Xa @ W3
            logits = Q @ W2 @ K.T / TAU
            n = logits.shape[1]
            order = jnp.argsort(-logits, axis=1)
            vals = jnp.take_along_axis(logits, order, axis=1)
            probs = jax.nn.softmax(vals, axis=1)
            csum = jnp.cumsum(probs, axis=1)
            k_i = jnp.sum(csum < P_TOP, axis=1) + 1
            keep = jnp.arange(n)[None, :] < k_i[:, None]
            masked_sorted = jnp.where(keep, vals, -jnp.inf)
            rows = jnp.arange(n)[:, None]
            masked = jnp.full_like(logits, -jnp.inf).at[rows, order].set(masked_sorted)
            return jax.nn.softmax(masked, axis=1)
        n = X.shape[0]
        S = S + jnp.eye(n, dtype=X.dtype)
        R = S / jnp.clip(S.sum(axis=1, keepdims=True), 1e-12)
        Z = jnp.zeros_like(X)
        Xf, Xa = (X, X)
        U1s, U2s = ((U1_0, U1_1), (U2_0, U2_1))
        for s in range(STEPS):
            A = _adj_from_feats(Xa, W1, W2, W3)
            Xf = R @ Xf
            Xa = A @ Xa
            Z = Z + (Xf @ U1s[s] + Xa @ U2s[s])
        Y = X + Z
        mu = Y.mean(axis=-1, keepdims=True)
        var = Y.var(axis=-1, keepdims=True)
        return (Y - mu) * jax.lax.rsqrt(var + LN_EPS) * gamma + beta

    def _L2_gnn_ref(x, adj, W, a1, a2, W1, b1, W2, b2, W3, b3, W4, b4):
        import jax, jax.numpy as jnp
        import numpy as np
        ALPHA = 0.2
        NEG = -9000000000000000.0
        N, NFEAT, NHID, NHEADS = (2048, 512, 64, 8)
        EMB = NHID * NHEADS
        Wh = jnp.einsum('nf,hfd->hnd', x, W)
        e_src = jnp.einsum('hnd,hd->hn', Wh, a1)
        e_dst = jnp.einsum('hnd,hd->hn', Wh, a2)
        e = jax.nn.leaky_relu(e_src[:, :, None] + e_dst[:, None, :], ALPHA)
        e = jnp.where(adj[None] > 0, e, NEG)
        att = jax.nn.softmax(e, axis=-1)
        h = jnp.einsum('hnm,hmd->hnd', att, Wh)
        h = jax.nn.elu(h)
        enc = jnp.transpose(h, (1, 0, 2)).reshape(x.shape[0], -1)
        out = jax.nn.relu(enc @ W1.T + b1)
        out = jax.nn.relu(out @ W2.T + b2)
        out = jax.nn.relu(out @ W3.T + b3)
        out = out @ W4.T + b4
        return out

    def _L3_gnn_ref(inst_feature, aggregator_matrix, rel_pair_index, Wq, bq, Wk, bk):
        import jax, jax.numpy as jnp
        import numpy as np
        N, H, E, HEADS = (1500, 512, 10000, 8)
        DK = H // HEADS
        n = inst_feature.shape[0]
        sub = rel_pair_index[:, 0]
        obj = rel_pair_index[:, 1]
        q = (inst_feature[sub] @ Wq.T + bq).reshape(-1, HEADS, DK)
        k = (inst_feature[obj] @ Wk.T + bk).reshape(-1, HEADS, DK)
        att = ((q * k).sum(-1) / np.sqrt(DK)).T.astype(inst_feature.dtype)
        scores = jnp.zeros((HEADS, n, n), dtype=inst_feature.dtype)
        scores = scores.at[:, sub, obj].set(att)
        mask = (1.0 - aggregator_matrix).astype(bool)
        scores = jnp.where(mask[None], -jnp.inf, scores)
        di = jnp.arange(n)
        scores = scores.at[:, di, di].set(1e-07)
        attn = jax.nn.softmax(scores, axis=2)
        aggregator_factor = attn.sum(axis=0) / HEADS
        return aggregator_factor @ inst_feature
    h = jnp.maximum(_layernorm(x, axis=-1), 0.0)
    x = x + _L0_gnn_ref(h, adj, L0_gnn_W_seq, L0_gnn_a1, L0_gnn_a2, L0_gnn_W_out, L0_gnn_b_out)
    h = jnp.maximum(_layernorm(x, axis=-1), 0.0)
    x = x + _L1_gnn_ref(h, adj, L1_gnn_W1, L1_gnn_W2, L1_gnn_W3, L1_gnn_U1_0, L1_gnn_U1_1, L1_gnn_U2_0, L1_gnn_U2_1, L1_gnn_gamma, L1_gnn_beta)
    h = jnp.maximum(_layernorm(x, axis=-1), 0.0)
    x = x + _L2_gnn_ref(h, adj, L2_gnn_W, L2_gnn_a1, L2_gnn_a2, L2_gnn_W1, L2_gnn_b1, L2_gnn_W2, L2_gnn_b2, L2_gnn_W3, L2_gnn_b3, L2_gnn_W4, L2_gnn_b4)
    h = jnp.maximum(_layernorm(x, axis=-1), 0.0)
    x = x + _L3_gnn_ref(h, adj, L3_gnn_rel_pair_index, L3_gnn_Wq, L3_gnn_bq, L3_gnn_Wk, L3_gnn_bk)
    return x

_drawn_inputs = setup_inputs


def setup_inputs(seed=0):
    import zlib

    import numpy as np

    out = dict(_drawn_inputs(seed))
    spreads = {'L1_gnn_gamma': (1.0, 0.2),
     'L1_gnn_beta': (0.0, 0.1),
     'L2_gnn_b1': (0.0, 0.8),
     'L2_gnn_b2': (0.0, 0.602),
     'L2_gnn_b3': (0.0, 0.1),
     'L2_gnn_b4': (0.0, 0.1),
     'L3_gnn_bq': (0.0, 2.0),
     'L3_gnn_bk': (0.0, 2.0)}
    factors = {'L0_gnn_b_out': 3.842,
     'L2_gnn_a1': 200.0,
     'L2_gnn_a2': 23.281,
     'L3_gnn_Wq': 200.0,
     'L3_gnn_Wk': 200.0}
    for name, (base, spread) in spreads.items():
        noise = np.random.default_rng([zlib.crc32(name.encode()), seed]).standard_normal(out[name].shape)
        drawn = base * np.exp(spread * noise) if base else spread * noise
        out[name] = jnp.asarray(drawn.astype(out[name].dtype))
    for name, factor in factors.items():
        out[name] = (out[name] * factor).astype(out[name].dtype)
    return out
```

```python
from contextlib import ExitStack, contextmanager

import concourse.bass as bass
from concourse import mybir

ALU = mybir.AluOpType
ACT = mybir.ActivationFunctionType
F32 = mybir.dt.float32
BF16 = mybir.dt.bfloat16
I32 = mybir.dt.int32
U32 = mybir.dt.uint32
AX = mybir.AxisListType

P = 128
N = 2048
D = 512
NT = N // P
KD = D // P
LN_EPS = 1e-5
SLOPE = 0.2
SHIFT = 20.0
STEEP = 2.0 ** 60
RING = 8
RELUS = 4
TOP_P = 0.9
BISECTIONS = 22
BIG = 1e30
REL_STD = 1e-7


class Count:

    def __init__(self, sem):
        self.sem, self.n = sem, 0

    def up(self, ins, by=1):
        ins.then_inc(self.sem, by)
        self.n += by
        return self.n


def chain(eng, sem):
    c = Count(sem)

    def link(ins):
        eng.wait_ge(sem, c.up(ins))

    return link


def tile(t):
    return slice(t * P, (t + 1) * P)


class Build:
    REL_HEADS = 8

    def __init__(self, nc, a, out):
        self.nc, self.a, self.out = nc, a, out
        self.names = 0
        self.owned = []

    @contextmanager
    def open(self):
        with ExitStack() as st:
            self.owned.append([])
            yield st
        sems = self.owned.pop()
        if sems:
            self.nc.clear_and_free_semaphores(sems)
            self.nc.all_engine_barrier()

    def sb(self, st, name, shape, dt=F32):
        return st.enter_context(self.nc.sbuf_tensor(self.unique(name), shape, dt))

    def ps(self, st, name, shape, dt=F32):
        return st.enter_context(self.nc.psum_tensor(self.unique(name), shape, dt))

    def sem(self, st, name):
        sem = self.nc.alloc_semaphore(self.unique(name))
        self.owned[-1].append(sem)
        return sem

    def unique(self, name):
        self.names += 1
        return f"{name}_{self.names}"

    def identity(self, pool, link, t):
        link(pool.memset(t[:, :], 0.0))
        link(pool.affine_select(out=t[:, :], in_=t[:, :], compare_op=ALU.not_equal, fill=1.0, base=0,
                                pattern=[[-1, P]], channel_multiplier=1))

    def norm_stage(self, x_dram, nat, tr, extra=None, transposed=True):
        nc = self.nc
        with self.open() as st:
            xs = self.sb(st, "xs", [P, NT, D])
            stats = self.sb(st, "stats", [P, NT, 6])
            mv = self.sb(st, "mv", [P, NT, 2])
            veps = self.sb(st, "veps", [P, NT])
            sd = self.sb(st, "sd", [P, NT])
            rstd = self.sb(st, "rstd", [P, NT])
            psT = self.ps(st, "psT", [P, 2, KD, P])
            x_in = [self.sem(st, f"x_in{c}") for c in range(4)]
            v_ready = self.sem(st, "v_ready")
            sd_ready = self.sem(st, "sd_ready")
            xn_ready = self.sem(st, "xn_ready")
            h_ready = self.sem(st, "h_ready")
            t_ready = self.sem(st, "t_ready")
            t_copied = self.sem(st, "t_copied")
            dve_done = self.sem(st, "dve_done")
            block = st.enter_context(nc.Block())

            @block.sync
            def _(sp):
                for c in range(4):
                    sp.dma_start(xs[:, 4 * c:4 * c + 4, :],
                                 x_dram[4 * c * P:4 * (c + 1) * P, :].rearrange("(t p) d -> p t d", p=P)
                                 ).then_inc(x_in[c], 16)

            @block.vector
            def _(dve):
                link = chain(dve, dve_done)
                for t in range(NT):
                    if t % 4 == 0:
                        dve.wait_ge(x_in[t // 4], 16)
                    last = dve.bn_stats(stats[:, t, :], xs[:, t, :])
                link(last)
                for t in range(NT):
                    last = dve.bn_aggr(mv[:, t, :], stats[:, t, :])
                link(last)
                dve.tensor_scalar(veps[:, :], mv[:, :, 1], LN_EPS, None, ALU.add).then_inc(v_ready, 1)
                dve.wait_ge(sd_ready, 1)
                link(dve.reciprocal(rstd[:, :], sd[:, :]))
                for t in range(NT):
                    dve.tensor_scalar(nat[:, t, :], xs[:, t, :], mv[:, t, 0:1], rstd[:, t:t + 1],
                                      ALU.subtract, ALU.mult).then_inc(xn_ready, 1)
                    if transposed and t >= 2:
                        dve.wait_ge(t_ready, t - 1)
                        dve.tensor_copy(tr[:, :, tile(t - 2)], psT[:, t % 2, :, :]).then_inc(t_copied, 1)
                if transposed:
                    for t in (NT - 2, NT - 1):
                        dve.wait_ge(t_ready, t + 1)
                        dve.tensor_copy(tr[:, :, tile(t)], psT[:, t % 2, :, :]).then_inc(t_copied, 1)

            @block.scalar
            def _(act):
                act.wait_ge(v_ready, 1)
                act.activation(sd[:, :], veps[:, :], ACT.Sqrt).then_inc(sd_ready, 1)
                for t in range(NT):
                    act.wait_ge(xn_ready, t + 1)
                    act.activation(nat[:, t, :], nat[:, t, :], ACT.Relu).then_inc(h_ready, 1)

            if transposed:
                @block.tensor
                def _(pe):
                    for t in range(NT):
                        pe.wait_ge(h_ready, t + 1)
                        if t >= 2:
                            pe.wait_ge(t_copied, t - 1)
                        for k in range(KD):
                            mm = pe.transpose(psT[:, t % 2, k, :], nat[:, t, tile(k)], self.ident[:, :])
                        mm.then_inc(t_ready, 1)

    def adjacency_stage(self):
        nc = self.nc
        with self.open() as st:
            rows = self.sb(st, "rows", [P, 2, N])
            rows16 = self.sb(st, "rows16", [P, 2, N], BF16)
            ident16 = self.sb(st, "ident16", [P, P], BF16)
            psT = self.ps(st, "psT", [P, 2, NT, P], BF16)
            adj_in = [self.sem(st, f"adj_in{c}") for c in range(2)]
            cast = self.sem(st, "cast")
            t_ready = self.sem(st, "t_ready")
            t_copied = self.sem(st, "t_copied")
            id_done = self.sem(st, "id_done")
            block = st.enter_context(nc.Block())

            @block.gpsimd
            def _(pool):
                link = chain(pool, id_done)
                self.identity(pool, link, self.ident)
                self.identity(pool, link, ident16)

            @block.sync
            def _(sp):
                for t in range(NT):
                    if t >= 2:
                        sp.wait_ge(cast, t - 1)
                    sp.dma_start(rows[:, t % 2, :], self.a["adj"][tile(t), :]).then_inc(adj_in[t % 2], 16)

            @block.vector
            def _(dve):
                for t in range(NT):
                    dve.wait_ge(adj_in[t % 2], 16 * (t // 2 + 1))
                    if t >= 2:
                        dve.wait_ge(t_ready, t - 1)
                    dve.tensor_copy(rows16[:, t % 2, :], rows[:, t % 2, :]).then_inc(cast, 1)

            @block.tensor
            def _(pe):
                pe.wait_ge(id_done, 4)
                for t in range(NT):
                    pe.wait_ge(cast, t + 1)
                    if t >= 2:
                        pe.wait_ge(t_copied, t - 1)
                    for j in range(NT):
                        mm = pe.transpose(psT[:, t % 2, j, :], rows16[:, t % 2, tile(j)], ident16[:, :])
                    mm.then_inc(t_ready, 1)

            @block.scalar
            def _(act):
                for t in range(NT):
                    act.wait_ge(t_ready, t + 1)
                    act.copy(self.adjT[:, :, tile(t)], psT[:, t % 2, :, :]).then_inc(t_copied, 1)

    def project_stage(self, H, DH, w_dram, a1_dram, a2_dram, seq, tr, g):
        nc = self.nc
        with self.open() as st:
            w = self.sb(st, "w", [P, KD, D])
            avec = self.sb(st, "avec", [P, 2, H, DH])
            prod = self.sb(st, "prod", [P, D])
            w12 = self.sb(st, "w12", [P, KD, 2, H])
            sT = self.sb(st, "sT", [2 * H, N])
            top = self.sb(st, "top", [2 * H, 1])
            m2 = self.sb(st, "m2", [P, H])
            s = self.sb(st, "s", [P, NT, 2, H])
            d2 = self.sb(st, "d2", [P, H, NT])
            c1 = self.sb(st, "c1", [P, H, NT])
            cmin = self.sb(st, "cmin", [P, H, NT])
            cmax = self.sb(st, "cmax", [P, H, NT])
            ftmp = self.sb(st, "ftmp", [P, H, NT])
            shift = self.sb(st, "shift", [P, 1])
            psQ = self.ps(st, "psQ", [P, 2, D])
            psS = self.ps(st, "psS", [P, 2, D])
            psR = self.ps(st, "psR", [P, N])
            w_in = self.sem(st, "w_in")
            a_in = self.sem(st, "a_in")
            w12_ready = self.sem(st, "w12_ready")
            seq_ready = self.sem(st, "seq_ready")
            seq_copied = self.sem(st, "seq_copied")
            s_ready = self.sem(st, "s_ready")
            s_copied = self.sem(st, "s_copied")
            sT_ready = self.sem(st, "sT_ready")
            sT_copied = self.sem(st, "sT_copied")
            sT_out = self.sem(st, "sT_out")
            top_ready = self.sem(st, "top_ready")
            top_out = self.sem(st, "top_out")
            m2_in = self.sem(st, "m2_in")
            args_ready = self.sem(st, "args_ready")
            exps_ready = self.sem(st, "exps_ready")
            dve_done = self.sem(st, "dve_done")
            block = st.enter_context(nc.Block())

            @block.sync
            def _(sp):
                if len(w_dram.shape) == 3:
                    for k in range(KD):
                        sp.dma_start(w[:, k, :].rearrange("p (h d) -> p h d", h=H),
                                     w_dram[:, tile(k), :].rearrange("h p d -> p h d")).then_inc(w_in, 16)
                else:
                    for k in range(KD):
                        sp.dma_start(w[:, k, :], w_dram[tile(k), :]).then_inc(w_in, 16)
                for i, v in enumerate((a1_dram, a2_dram)):
                    if len(v.shape) == 1:
                        for h in range(H):
                            sp.dma_start(avec[:, i, h, :], v.partition_broadcast(P)).then_inc(a_in, 16)
                    else:
                        sp.dma_start(avec[:, i, :, :], v.partition_broadcast(P)).then_inc(a_in, 16)
                sp.wait_ge(sT_copied, 4)
                sp.dma_start(g.sT_dram[0:2 * H, :], sT[:, :]).then_inc(sT_out, 16)
                sp.wait_ge(top_ready, 1)
                sp.dma_start(g.top_dram[0:2 * H].rearrange("(h o) -> h o", o=1), top[:, :]).then_inc(top_out, 16)
                sp.wait_ge(top_out, 16)
                sp.dma_start(m2[:, :], g.top_dram[H:2 * H].partition_broadcast(P)).then_inc(m2_in, 16)
                sp.wait_ge(sT_out, 16)

            n_a = sum(H if len(v.shape) == 1 else 1 for v in (a1_dram, a2_dram))

            @block.vector
            def _(dve):
                link = chain(dve, dve_done)
                dve.wait_ge(w_in, 16 * KD)
                dve.wait_ge(a_in, 16 * n_a)
                for k in range(KD):
                    for i in range(2):
                        link(dve.tensor_tensor(prod[:, :], w[:, k, :],
                                               avec[:, i, :, :].rearrange("p h d -> p (h d)"), ALU.mult))
                        link(dve.tensor_reduce(w12[:, k, i, :], prod[:, :].rearrange("p (h d) -> p h d", h=H),
                                               AX.X, ALU.add))
                dve.memset(shift[:, :], SHIFT).then_inc(w12_ready, 1)
                for t in range(NT):
                    dve.wait_ge(s_ready, t + 1)
                    dve.tensor_copy(s[:, t, :, :].rearrange("p i h -> p (i h)"),
                                    psS[:, t % 2, 0:2 * H]).then_inc(s_copied, 1)
                dve.wait_ge(sT_copied, 4)
                dve.tensor_reduce(top[:, :], sT[:, :], AX.X, ALU.max).then_inc(top_ready, 1)
                dve.wait_ge(s_copied, NT)
                dve.wait_ge(m2_in, 16)
                s1 = s[:, :, 0, :].rearrange("p t h -> p h t")
                s2 = s[:, :, 1, :].rearrange("p t h -> p h t")
                m2b = m2[:, :].unsqueeze(2).to_broadcast([P, H, NT])
                dve.tensor_tensor(d2[:, :, :], s2, m2b, ALU.subtract)
                dve.tensor_scalar(g.thr[:, :, :], s2, -1.0, None, ALU.mult)
                dve.tensor_scalar(g.steep[:, :, :], s2, STEEP, None, ALU.mult)
                link(dve.tensor_tensor(c1[:, :, :], s1, m2b, ALU.add))
                dve.tensor_scalar(cmin[:, :, :], c1[:, :, :], 0.0, 1.0 - SLOPE, ALU.min, ALU.mult)
                dve.tensor_scalar(cmax[:, :, :], c1[:, :, :], 0.0, SLOPE - 1.0, ALU.max,
                                  ALU.mult).then_inc(args_ready, 1)
                dve.wait_ge(exps_ready, 1)
                dve.tensor_scalar(g.colF[:, :, :], ftmp[:, :, :], -1.0, None, ALU.mult)

            @block.scalar
            def _(act):
                for t in range(NT):
                    act.wait_ge(seq_ready, t + 1)
                    act.copy(seq[:, t, :], psQ[:, t % 2, :]).then_inc(seq_copied, 1)
                for c in range(4):
                    act.wait_ge(sT_ready, c + 1)
                    act.copy(sT[:, c * D:(c + 1) * D], psR[0:2 * H, c * D:(c + 1) * D]).then_inc(sT_copied, 1)
                act.wait_ge(args_ready, 1)
                act.activation(g.colE[:, :, :], d2[:, :, :], ACT.Exp, bias=shift[:, 0:1])
                act.activation(g.rowE[:, :, :], cmin[:, :, :], ACT.Exp)
                act.activation(g.rowF[:, :, :], cmax[:, :, :], ACT.Exp)
                act.activation(ftmp[:, :, :], d2[:, :, :], ACT.Exp, bias=shift[:, 0:1],
                               scale=SLOPE).then_inc(exps_ready, 1)

            @block.tensor
            def _(pe):
                pe.wait_ge(w_in, 16 * KD)
                for t in range(NT):
                    if t >= 2:
                        pe.wait_ge(seq_copied, t - 1)
                    for k in range(KD):
                        mm = pe.matmul(psQ[:, t % 2, :], tr[:, k, tile(t)], w[:, k, :],
                                       start=(k == 0), stop=(k == KD - 1))
                    mm.then_inc(seq_ready, 1)
                pe.wait_ge(w12_ready, 1)
                for t in range(NT):
                    if t >= 2:
                        pe.wait_ge(s_copied, t - 1)
                    for k in range(KD):
                        mm = pe.matmul(psS[:, t % 2, 0:2 * H], tr[:, k, tile(t)],
                                       w12[:, k, :, :].rearrange("p i h -> p (i h)"),
                                       start=(k == 0), stop=(k == KD - 1))
                    mm.then_inc(s_ready, 1)
                for c in range(4):
                    for k in range(KD):
                        mm = pe.matmul(psR[0:2 * H, c * D:(c + 1) * D],
                                       w12[:, k, :, :].rearrange("p i h -> p (i h)"),
                                       tr[:, k, c * D:(c + 1) * D], start=(k == 0), stop=(k == KD - 1))
                    mm.then_inc(sT_ready, 1)

    def attention_stage(self, H, DH, IB, relu_tiles, seq, hid, g):
        nc = self.nc
        C = DH + 1
        W = 3 * C
        NC = NT // IB
        CI = IB * P
        TB = 512 // (2 * W)
        SH = NC * NT
        RK = len(relu_tiles)
        HJ = NT // 2
        relu_at = {j: k for k, j in enumerate(relu_tiles)}
        assert IB == 4 * TB and (2 * NC) % 4 == 0
        with self.open() as st:
            s1b = self.sb(st, "s1b", [P, 4, CI])
            mask = self.sb(st, "mask", [P, RING, CI], BF16)
            steepz = self.sb(st, "steepz", [P, RELUS, CI], BF16)
            V = self.sb(st, "V", [P, 2, NT, 3, W], BF16)
            Vs = self.sb(st, "Vs", [P, HJ, 2, C])
            thr_h = self.sb(st, "thr_h", [P, 2, 2, NT])
            sums = self.sb(st, "sums", [P, IB, 2, C])
            wsum = self.sb(st, "wsum", [P, IB, 2, C])
            num = self.sb(st, "num", [P, IB, C])
            rec = self.sb(st, "rec", [P, IB])
            acc = self.ps(st, "acc", [P, 2, 4, 512])
            s1b_in = [self.sem(st, f"s1b_in{q}") for q in range(4)]
            thr_ready = self.sem(st, "thr_ready")
            V_ready = self.sem(st, "V_ready")
            relu_ready = self.sem(st, "relu_ready")
            mask_ready = self.sem(st, "mask_ready")
            mask_used = self.sem(st, "mask_used")
            acc_ready = self.sem(st, "acc_ready")
            acc_free = self.sem(st, "acc_free")
            dve_done = self.sem(st, "dve_done")
            block = st.enter_context(nc.Block())
            N_COLS, N_RES = 2 * 7 + 1, 8

            def pairs(eng, body):
                body(0, True)
                with eng.Fori(1, H // 2) as pair:
                    body(pair * 2, False)

            @block.sync
            def _(sp):
                def body(h0, first):
                    for u in range(2):
                        for c in range(NC):
                            q = u * NC + c
                            if not first or q >= 4:
                                sp.wait_ge(mask_ready, h0 * SH + (q - 3) * NT)
                            sp.dma_start(s1b[:, q % 4, :],
                                         g.sT_dram[bass.ds(h0 + u, 1), c * CI:(c + 1) * CI]
                                         .rearrange("o n -> (o n)").partition_broadcast(P)
                                         ).then_inc(s1b_in[q % 4], 16)
                pairs(sp, body)

            @block.scalar
            def _(act):
                def body(h0, first):
                    for u in range(2):
                        act.wait_ge(thr_ready, h0 + u + 1)
                        for c in range(NC):
                            q = u * NC + c
                            act.wait_ge(s1b_in[q % 4], h0 * (NC * 4) + 16 * (q // 4 + 1))
                            for j in relu_tiles:
                                k = relu_at[j]
                                m = q * RK + k
                                if not first or m >= RELUS:
                                    back = m - RELUS
                                    n = (back // RK) * NT + relu_tiles[back % RK]
                                    act.wait_ge(mask_ready, h0 * SH + n + 1)
                                act.activation(steepz[:, m % RELUS, :], s1b[:, q % 4, :], ACT.Relu,
                                               bias=thr_h[:, u, 1, j:j + 1], scale=STEEP
                                               ).then_inc(relu_ready, 1)
                pairs(act, body)

            @block.vector
            def _(dve):
                base = [0, 0]

                def link(ins):
                    base[1] += 1
                    ins.then_inc(dve_done, 1)
                    dve.wait_ge(dve_done, base[0] + base[1])

                def columns(h, u):
                    dve.tensor_copy(thr_h[:, u, 0, :], g.thr[:, bass.ds(h, 1), :].rearrange("p o t -> p (o t)"))
                    ins = dve.tensor_copy(thr_h[:, u, 1, :], g.steep[:, bass.ds(h, 1), :].rearrange("p o t -> p (o t)"))
                    ins.then_inc(thr_ready, 1)
                    for half in range(2):
                        js = slice(half * HJ, (half + 1) * HJ)
                        sq = seq[:, js, bass.ds(h * DH, DH)]
                        cE = g.colE[:, bass.ds(h, 1), js].rearrange("p o t -> p (o t)")
                        cF = g.colF[:, bass.ds(h, 1), js].rearrange("p o t -> p (o t)")
                        dve.tensor_tensor(Vs[:, :, 0, 0:DH], sq, cE.unsqueeze(2).to_broadcast([P, HJ, DH]), ALU.mult)
                        dve.tensor_tensor(Vs[:, :, 1, 0:DH], sq, cF.unsqueeze(2).to_broadcast([P, HJ, DH]), ALU.mult)
                        dve.tensor_copy(Vs[:, :, 0, DH:C].rearrange("p t o -> p (t o)"), cE)
                        link(dve.tensor_copy(Vs[:, :, 1, DH:C].rearrange("p t o -> p (t o)"), cF))
                        for part in range(3):
                            pt = V[:, u, js, 0:2, part * C:(part + 1) * C]
                            link(dve.tensor_copy(pt, Vs[:, :, :, :]))
                            if part < 2:
                                link(dve.tensor_tensor(Vs[:, :, :, :], Vs[:, :, :, :], pt, ALU.subtract))
                        ins = dve.tensor_scalar(V[:, u, js, 2, :], V[:, u, js, 1, :], -1.0, None, ALU.mult)
                        if half == 0:
                            link(ins)
                        else:
                            ins.then_inc(V_ready, 1)
                    dve.wait_ge(thr_ready, h + 1)
                    link(dve.memset(rec[:, 0:1], 1.0))

                def results(h, c, n):
                    b = c % 2
                    dve.wait_ge(acc_ready, n + 1)
                    for bank in range(4):
                        ins = dve.tensor_reduce(
                            sums[:, bank * TB:(bank + 1) * TB, :, :].rearrange("p t s c -> p (t s) c"),
                            acc[:, b, bank, 0:TB * 2 * W].rearrange("p (x r c) -> p x c r", r=3, c=C),
                            AX.X, ALU.add)
                        if bank == 3:
                            ins.then_inc(acc_free, 1)
                    dve.wait_ge(acc_free, n + 1)
                    rE = g.rowE[:, bass.ds(h, 1), c * IB:(c + 1) * IB].rearrange("p o t -> p (o t)")
                    rF = g.rowF[:, bass.ds(h, 1), c * IB:(c + 1) * IB].rearrange("p o t -> p (o t)")
                    dve.tensor_tensor(wsum[:, :, 0, :], sums[:, :, 0, :], rE.unsqueeze(2).to_broadcast([P, IB, C]), ALU.mult)
                    link(dve.tensor_tensor(wsum[:, :, 1, :], sums[:, :, 1, :], rF.unsqueeze(2).to_broadcast([P, IB, C]), ALU.mult))
                    link(dve.tensor_tensor(num[:, :, :], wsum[:, :, 0, :], wsum[:, :, 1, :], ALU.add))
                    link(dve.reciprocal(rec[:, :], num[:, :, DH]))
                    link(dve.tensor_tensor(hid[:, c * IB:(c + 1) * IB, bass.ds(h * DH, DH)], num[:, :, 0:DH],
                                           rec[:, :].unsqueeze(2).to_broadcast([P, IB, DH]), ALU.mult))

                per_pair = [None]

                def body(h0, first):
                    base[0] = 0 if first else h0 * (per_loop // 2) - per_chunk
                    base[1] = 0
                    for u in range(2):
                        columns(h0 + u, u)
                        for c in range(NC):
                            q = u * NC + c
                            dve.wait_ge(s1b_in[q % 4], h0 * (NC * 4) + 16 * (q // 4 + 1))
                            for j in range(NT):
                                n = q * NT + j
                                if not first or n >= RING:
                                    dve.wait_ge(mask_used, h0 * SH + n - RING + 1)
                                out = mask[:, j % RING, :]
                                adj = self.adjT[:, j, c * CI:(c + 1) * CI]
                                if j in relu_at:
                                    m = q * RK + relu_at[j]
                                    dve.wait_ge(relu_ready, h0 * (NC * RK) + m + 1)
                                    dve.tensor_tensor(out, steepz[:, m % RELUS, :], adj, ALU.min).then_inc(mask_ready, 1)
                                else:
                                    dve.scalar_tensor_tensor(out, s1b[:, q % 4, :], thr_h[:, u, 0, j:j + 1], adj,
                                                             ALU.is_gt, ALU.mult).then_inc(mask_ready, 1)
                                if j == RING + 1 and (not first or q >= 1):
                                    hh = h0 + u if c >= 1 else h0 + u - 1
                                    results(hh, (c - 1) % NC, h0 * NC + q - 1)
                    return base[1]

                per_chunk = 4
                per_head = 2 * 7 + per_chunk * NC
                in_first = 2 * per_head - per_chunk
                per_loop = 2 * per_head
                assert body(0, True) == in_first
                with dve.Fori(1, H // 2) as pair:
                    assert body(pair * 2, False) == per_loop
                base[0], base[1] = in_first + (H - 2) // 2 * per_loop, 0
                results(H - 1, NC - 1, H * NC - 1)

            @block.tensor
            def _(pe):
                def body(h0, first):
                    for u in range(2):
                        pe.wait_ge(V_ready, h0 + u + 1)
                        for c in range(NC):
                            q = u * NC + c
                            if not first or q >= 2:
                                pe.wait_ge(acc_free, h0 * NC + q - 1)
                            for j in range(NT):
                                n = q * NT + j
                                pe.wait_ge(mask_ready, h0 * SH + n + 1)
                                for i in range(IB):
                                    o = (i % TB) * 2 * W
                                    mm = pe.matmul(acc[:, c % 2, i // TB, o:o + 2 * W], mask[:, j % RING, tile(i)],
                                                   V[:, u, j, 0:2, :].rearrange("p s w -> p (s w)"),
                                                   start=(j == 0 and i % TB == 0), stop=False,
                                                   skip_group_check=True)
                                mm.then_inc(mask_used, 1)
                                for i in range(IB):
                                    o = (i % TB) * 2 * W + W
                                    mm = pe.matmul(acc[:, c % 2, i // TB, o:o + W],
                                                   self.adjT[:, j, tile(c * IB + i)], V[:, u, j, 2, :],
                                                   start=False, stop=(j == NT - 1 and i % TB == TB - 1),
                                                   skip_group_check=True)
                            mm.then_inc(acc_ready, 1)
                pairs(pe, body)

    def transpose_tiles(self, pe, psT, t, nat, ready, free, n0=0):
        if t >= 2:
            pe.wait_ge(free, n0 + t - 1)
        for k in range(KD):
            mm = pe.transpose(psT[:, t % 2, k, :], nat[:, t, tile(k)], self.ident[:, :])
        mm.then_inc(ready, 1)

    def elu_out_stage(self, nat, tr, w_dram, b_dram, x_dram, x_new):
        nc = self.nc
        with self.open() as st:
            w = self.sb(st, "w", [P, KD, D])
            bias = self.sb(st, "bias", [P, D])
            xt = self.sb(st, "xt", [P, 4, D])
            v = self.sb(st, "v", [P, 2, D])
            neg = self.sb(st, "neg", [P, 2, D])
            y = self.sb(st, "y", [P, 2, D])
            xo = self.sb(st, "xo", [P, 4, D])
            psT = self.ps(st, "psT", [P, 2, KD, P])
            psO = self.ps(st, "psO", [P, 2, D])
            w_in = self.sem(st, "w_in")
            x_in = [self.sem(st, f"x_in{i}") for i in range(4)]
            x_out = [self.sem(st, f"x_out{i}") for i in range(4)]
            t_ready = self.sem(st, "t_ready")
            t_copied = self.sem(st, "t_copied")
            o_ready = self.sem(st, "o_ready")
            v_ready = self.sem(st, "v_ready")
            neg_ready = self.sem(st, "neg_ready")
            exp_ready = self.sem(st, "exp_ready")
            y_ready = self.sem(st, "y_ready")
            x_ready = self.sem(st, "x_ready")
            block = st.enter_context(nc.Block())

            @block.sync
            def _(sp):
                for k in range(KD):
                    sp.dma_start(w[:, k, :], w_dram[tile(k), :]).then_inc(w_in, 16)
                sp.dma_start(bias[:, :], b_dram.partition_broadcast(P)).then_inc(w_in, 16)
                for t in range(NT):
                    if t >= 4:
                        sp.wait_ge(x_ready, t - 3)
                    sp.dma_start(xt[:, t % 4, :], x_dram[tile(t), :]).then_inc(x_in[t % 4], 16)

            @block.gpsimd
            def _(pool):
                for t in range(NT):
                    pool.wait_ge(x_ready, t + 1)
                    pool.dma_start(x_new[tile(t), :], xo[:, t % 4, :]).then_inc(x_out[t % 4], 16)
                for i in range(4):
                    pool.wait_ge(x_out[i], 16 * (NT // 4))

            @block.tensor
            def _(pe):
                for t in range(NT):
                    self.transpose_tiles(pe, psT, t, nat, t_ready, t_copied)
                pe.wait_ge(w_in, 16 * (KD + 1))
                for t in range(NT):
                    pe.wait_ge(t_copied, t + 1)
                    if t >= 2:
                        pe.wait_ge(v_ready, t - 1)
                    for k in range(KD):
                        mm = pe.matmul(psO[:, t % 2, :], tr[:, k, tile(t)], w[:, k, :],
                                       start=(k == 0), stop=(k == KD - 1))
                    mm.then_inc(o_ready, 1)

            @block.scalar
            def _(act):
                for t in range(NT):
                    act.wait_ge(t_ready, t + 1)
                    act.copy(tr[:, :, tile(t)], psT[:, t % 2, :, :]).then_inc(t_copied, 1)
                for t in range(NT):
                    act.wait_ge(neg_ready, t + 1)
                    act.activation(neg[:, t % 2, :], neg[:, t % 2, :], ACT.Exp).then_inc(exp_ready, 1)

            @block.vector
            def _(dve):
                dve.wait_ge(w_in, 16 * (KD + 1))

                def finish(t):
                    dve.wait_ge(exp_ready, t + 1)
                    dve.scalar_tensor_tensor(y[:, t % 2, :], v[:, t % 2, :], 0.0, neg[:, t % 2, :],
                                             ALU.max, ALU.add).then_inc(y_ready, 1)
                    dve.wait_ge(x_in[t % 4], 16 * (t // 4 + 1))
                    if t >= 4:
                        dve.wait_ge(x_out[t % 4], 16 * (t // 4))
                    dve.wait_ge(y_ready, t + 1)
                    dve.scalar_tensor_tensor(xo[:, t % 4, :], y[:, t % 2, :], -1.0, xt[:, t % 4, :],
                                             ALU.add, ALU.add).then_inc(x_ready, 1)

                for t in range(NT):
                    if t >= 2:
                        dve.wait_ge(x_ready, t - 1)
                    dve.wait_ge(o_ready, t + 1)
                    dve.tensor_tensor(v[:, t % 2, :], psO[:, t % 2, :], bias[:, :], ALU.add).then_inc(v_ready, 1)
                    dve.wait_ge(v_ready, t + 1)
                    dve.tensor_scalar(neg[:, t % 2, :], v[:, t % 2, :], 0.0, None, ALU.min).then_inc(neg_ready, 1)
                    if t >= 1:
                        finish(t - 1)
                finish(NT - 1)

    def weight_transpose_stage(self, items):
        nc = self.nc
        with self.open() as st:
            loads = [self.sb(st, "wn", [P, w.shape[0] // P, w.shape[1]]) for w, _ in items]
            psT = self.ps(st, "psT", [P, 4, 512])
            w_in = [self.sem(st, "w_in") for _ in items]
            t_ready = self.sem(st, "t_ready")
            t_copied = self.sem(st, "t_copied")
            blocks = [(n, r, c) for n, (w, _) in enumerate(items)
                      for r in range(w.shape[0] // P) for c in range(w.shape[1] // P)]
            block = st.enter_context(nc.Block())

            @block.sync
            def _(sp):
                for n, (w, _) in enumerate(items):
                    sp.dma_start(loads[n][:, :, :], w.rearrange("(r p) c -> p r c", p=P)).then_inc(w_in[n], 16)

            @block.tensor
            def _(pe):
                for i, (n, r, c) in enumerate(blocks):
                    pe.wait_ge(w_in[n], 16)
                    if i >= 4:
                        pe.wait_ge(t_copied, i - 3)
                    pe.transpose(psT[:, i % 4, 0:P], loads[n][:, r, tile(c)], self.ident[:, :]).then_inc(t_ready, 1)

            @block.scalar
            def _(act):
                for i, (n, r, c) in enumerate(blocks):
                    act.wait_ge(t_ready, i + 1)
                    act.copy(items[n][1][:, c, tile(r)], psT[:, i % 4, 0:P]).then_inc(t_copied, 1)

    def mlp_stage(self, nat, tr, x_dram, x_new):
        nc, a = self.nc, self.a
        E1, E2, E3 = a["L2_gnn_W1"].shape[0] // P, a["L2_gnn_W2"].shape[0] // P, a["L2_gnn_W3"].shape[0] // P
        with self.open() as st:
            w1t = self.sb(st, "w1t", [P, KD, E1 * P])
            w2t = self.sb(st, "w2t", [P, E1, E2 * P])
            w3t = self.sb(st, "w3t", [P, E2, E3 * P])
            w4t = self.sb(st, "w4t", [P, E3, D])
            self.weight_transpose_stage([(a["L2_gnn_W1"], w1t), (a["L2_gnn_W2"], w2t),
                                         (a["L2_gnn_W3"], w3t), (a["L2_gnn_W4"], w4t)])
            b1 = self.sb(st, "b1", [P, E1])
            b2 = self.sb(st, "b2", [P, E2])
            b3 = self.sb(st, "b3", [P, E3])
            b4 = self.sb(st, "b4", [P, D])
            neg = self.sb(st, "neg", [P, 2, D])
            y1 = self.sb(st, "y1", [P, E1, N])
            y2 = self.sb(st, "y2", [P, E2, N])
            xt = self.sb(st, "xt", [P, 4, D])
            xo = self.sb(st, "xo", [P, 4, D])
            psT = self.ps(st, "psT", [P, 2, KD, P])
            psL = self.ps(st, "psL", [P, 2, 512])
            psO = self.ps(st, "psO", [P, 2, D])
            b_in = self.sem(st, "b_in")
            x_in = [self.sem(st, f"x_in{i}") for i in range(4)]
            x_out = [self.sem(st, f"x_out{i}") for i in range(4)]
            neg_ready = self.sem(st, "neg_ready")
            exp_ready = self.sem(st, "exp_ready")
            elu_ready = self.sem(st, "elu_ready")
            t_ready = self.sem(st, "t_ready")
            t_copied = self.sem(st, "t_copied")
            l_ready = self.sem(st, "l_ready")
            l_done = self.sem(st, "l_done")
            o_ready = self.sem(st, "o_ready")
            v_ready = self.sem(st, "v_ready")
            x_ready = self.sem(st, "x_ready")
            block = st.enter_context(nc.Block())
            y3 = nat.rearrange("p t d -> p (t d)")[:, 0:E3 * N].rearrange("p (e n) -> p e n", e=E3)
            layers = [(w1t, tr, b1, y1, KD, E1), (w2t, y1, b2, y2, E1, E2), (w3t, y2, b3, y3, E2, E3)]
            steps = [(l, m, c) for l in range(3) for m in range(layers[l][5]) for c in range(N // 512)]
            ends = [sum(layers[l][5] for l in range(n)) * (N // 512) for n in range(4)]

            @block.sync
            def _(sp):
                for t_, v in ((b1, "L2_gnn_b1"), (b2, "L2_gnn_b2"), (b3, "L2_gnn_b3")):
                    sp.dma_start(t_[:, :], a[v].rearrange("(e p) -> p e", p=P),
                                 allow_slow_non_contiguous=True).then_inc(b_in, 16)
                sp.dma_start(b4[:, :], a["L2_gnn_b4"].partition_broadcast(P)).then_inc(b_in, 16)
                for t in range(NT):
                    if t >= 4:
                        sp.wait_ge(x_ready, t - 3)
                    sp.dma_start(xt[:, t % 4, :], x_dram[tile(t), :]).then_inc(x_in[t % 4], 16)

            @block.gpsimd
            def _(pool):
                for t in range(NT):
                    pool.wait_ge(x_ready, t + 1)
                    pool.dma_start(x_new[tile(t), :], xo[:, t % 4, :]).then_inc(x_out[t % 4], 16)
                for i in range(4):
                    pool.wait_ge(x_out[i], 16 * (NT // 4))

            @block.vector
            def _(dve):
                def elu(t):
                    dve.wait_ge(exp_ready, t + 1)
                    dve.scalar_tensor_tensor(nat[:, t, :], nat[:, t, :], 0.0, neg[:, t % 2, :],
                                             ALU.max, ALU.add).then_inc(elu_ready, 1)

                for t in range(NT):
                    if t >= 2:
                        dve.wait_ge(elu_ready, t - 1)
                    dve.tensor_scalar(neg[:, t % 2, :], nat[:, t, :], 0.0, None, ALU.min).then_inc(neg_ready, 1)
                    if t >= 1:
                        elu(t - 1)
                elu(NT - 1)
                for t in range(NT):
                    dve.wait_ge(t_ready, t + 1)
                    dve.tensor_scalar(tr[:, :, tile(t)], psT[:, t % 2, :, :], -1.0, None,
                                      ALU.add).then_inc(t_copied, 1)
                dve.wait_ge(b_in, 64)
                for t in range(NT):
                    dve.wait_ge(o_ready, t + 1)
                    if t >= 4:
                        dve.wait_ge(x_out[t % 4], 16 * (t // 4))
                    dve.tensor_tensor(xo[:, t % 4, :], psO[:, t % 2, :], b4[:, :], ALU.add).then_inc(v_ready, 1)
                    dve.wait_ge(x_in[t % 4], 16 * (t // 4 + 1))
                    dve.wait_ge(v_ready, t + 1)
                    dve.tensor_tensor(xo[:, t % 4, :], xo[:, t % 4, :], xt[:, t % 4, :],
                                      ALU.add).then_inc(x_ready, 1)

            @block.scalar
            def _(act):
                for t in range(NT):
                    act.wait_ge(neg_ready, t + 1)
                    act.activation(neg[:, t % 2, :], neg[:, t % 2, :], ACT.Exp).then_inc(exp_ready, 1)
                act.wait_ge(b_in, 64)
                act.wait_ge(t_ready, NT)
                for i, (l, m, c) in enumerate(steps):
                    act.wait_ge(l_ready, i + 1)
                    act.activation(layers[l][3][:, m, c * 512:(c + 1) * 512], psL[:, i % 2, :], ACT.Relu,
                                   bias=layers[l][2][:, m:m + 1]).then_inc(l_done, 1)

            @block.tensor
            def _(pe):
                for t in range(NT):
                    pe.wait_ge(elu_ready, t + 1)
                    self.transpose_tiles(pe, psT, t, nat, t_ready, t_copied)
                pe.wait_ge(t_copied, NT)
                for i, (l, m, c) in enumerate(steps):
                    w, x, _, _, kk, _ = layers[l]
                    if max(ends[l], i - 1) > 0:
                        pe.wait_ge(l_done, max(ends[l], i - 1))
                    for k in range(kk):
                        mm = pe.matmul(psL[:, i % 2, :], w[:, k, tile(m)], x[:, k, c * 512:(c + 1) * 512],
                                       start=(k == 0), stop=(k == kk - 1))
                    mm.then_inc(l_ready, 1)
                pe.wait_ge(l_done, ends[3])
                for t in range(NT):
                    if t >= 2:
                        pe.wait_ge(v_ready, t - 1)
                    for k in range(E3):
                        mm = pe.matmul(psO[:, t % 2, :], y3[:, k, tile(t)], w4t[:, k, :],
                                       start=(k == 0), stop=(k == E3 - 1))
                    mm.then_inc(o_ready, 1)

    def diffusion_stage(self, X, Xflat, F, x_dram, y_dram):
        nc, a = self.nc, self.a
        self.norm_stage(x_dram, X, None, transposed=False)
        with self.open() as st:
            parts = self.sb(st, "parts", [P, NT, 3, D], BF16)
            rest = self.sb(st, "rest", [P, 2, D])
            ones = self.sb(st, "ones", [P, 2], BF16)
            deg = self.sb(st, "deg", [P, NT])
            rinv = self.sb(st, "rinv", [P, NT])
            E = a["L3_gnn_rel_pair_index"].shape[0]
            R = next(r for r in range(P, 0, -1) if E % r == 0)
            self.rel_bufs = (self.sb(st, "zeros", [P, 256]), self.sb(st, "pairs", [P, E // R, 2], I32),
                             self.sb(st, "index", [P, E // R], I32), self.sb(st, "relone", [P, 1]))
            self.rel_sems = {n: self.sem(st, "rel_" + n) for n in ("ready", "in", "cleared", "marked")}
            w = self.sb(st, "w", [P, 2, KD, D])
            f2 = self.sb(st, "f2", [P, 2, D])
            fT = self.sb(st, "fT", [P, 2, KD, P])
            psF = self.ps(st, "psF", [P, 2, D])
            psD = self.ps(st, "psD", [P, 512])
            psT = self.ps(st, "psT", [P, 2, KD, P])
            psY = self.ps(st, "psY", [P, 2, D])
            w_in = self.sem(st, "w_in")
            part_ready = self.sem(st, "part_ready")
            dve_done = self.sem(st, "dve_done")
            ones_ready = self.sem(st, "ones_ready")
            deg_ready = self.sem(st, "deg_ready")
            rinv_ready = self.sem(st, "rinv_ready")
            f_ready = self.sem(st, "f_ready")
            f_copied = self.sem(st, "f_copied")
            t_ready = self.sem(st, "t_ready")
            t_copied = self.sem(st, "t_copied")
            y_ready = self.sem(st, "y_ready")
            y_copied = self.sem(st, "y_copied")
            y_out = [self.sem(st, f"y_out{i}") for i in range(2)]
            block = st.enter_context(nc.Block())

            @block.gpsimd
            def _(pool):
                self.relation_table(pool, st, self.table)

            @block.sync
            def _(sp):
                for s, name in enumerate(("L1_gnn_U1_0", "L1_gnn_U1_1")):
                    for k in range(KD):
                        sp.dma_start(w[:, s, k, :], a[name][tile(k), :]).then_inc(w_in, 16)
                for t in range(NT):
                    sp.wait_ge(y_copied, t + 1)
                    sp.dma_start(y_dram[tile(t), :], F[:, t, :]).then_inc(y_out[t % 2], 16)
                for i in range(2):
                    sp.wait_ge(y_out[i], 16 * (NT // 2))

            @block.vector
            def _(dve):
                link = chain(dve, dve_done)

                def split(src):
                    for t in range(NT):
                        link(dve.tensor_copy(parts[:, t, 0, :], src[:, t, :]))
                        link(dve.tensor_tensor(rest[:, 0, :], src[:, t, :], parts[:, t, 0, :], ALU.subtract))
                        link(dve.tensor_copy(parts[:, t, 1, :], rest[:, 0, :]))
                        link(dve.tensor_tensor(rest[:, 1, :], rest[:, 0, :], parts[:, t, 1, :], ALU.subtract))
                        dve.tensor_copy(parts[:, t, 2, :], rest[:, 1, :]).then_inc(part_ready, 1)
                        dve.wait_ge(part_ready, (t + 1) if src is X else NT + t + 1)

                def residual(t):
                    dve.wait_ge(y_ready, t + 1)
                    dve.tensor_tensor(F[:, t, :], psY[:, t % 2, :], X[:, t, :], ALU.add).then_inc(y_copied, 1)

                link(dve.memset(ones[:, :], 1.0))
                dve.memset(rest[:, 0, 0:1], 0.0).then_inc(ones_ready, 1)
                dve.wait_ge(ones_ready, 1)
                split(X)
                dve.wait_ge(deg_ready, 1)
                link(dve.tensor_scalar(deg[:, :], psD[:, 0:NT], 1.0, 1e-12, ALU.add, ALU.max))
                dve.reciprocal(rinv[:, :], deg[:, :]).then_inc(rinv_ready, 1)
                dve.wait_ge(rinv_ready, 1)
                for t in range(NT):
                    dve.wait_ge(f_ready, t + 1)
                    link(dve.tensor_tensor(rest[:, 0, :], psF[:, t % 2, :], X[:, t, :], ALU.add))
                    dve.tensor_scalar(F[:, t, :], rest[:, 0, :], rinv[:, t:t + 1], None,
                                      ALU.mult).then_inc(f_copied, 1)
                    dve.wait_ge(f_copied, t + 1)
                split(F)
                for t in range(NT):
                    dve.wait_ge(f_ready, NT + t + 1)
                    link(dve.tensor_tensor(rest[:, 0, :], psF[:, t % 2, :], F[:, t, :], ALU.add))
                    if t >= 2:
                        dve.wait_ge(t_ready, 2 * (t - 1))
                    dve.tensor_scalar(f2[:, t % 2, :], rest[:, 0, :], rinv[:, t:t + 1], None,
                                      ALU.mult).then_inc(f_copied, 1)
                    dve.wait_ge(f_copied, NT + t + 1)
                    if t >= 1:
                        residual(t - 1)
                residual(NT - 1)

            @block.scalar
            def _(act):
                for t in range(2 * NT):
                    act.wait_ge(t_ready, t + 1)
                    if t >= 2:
                        act.wait_ge(y_ready, t // 2)
                    act.copy(fT[:, t % 2, :, :], psT[:, t % 2, :, :]).then_inc(t_copied, 1)

            @block.tensor
            def _(pe):
                def spread(s, t):
                    n = s * NT + t
                    if n >= 2:
                        pe.wait_ge(f_copied, n - 1)
                    for j in range(NT):
                        if t == 0:
                            pe.wait_ge(part_ready, s * NT + j + 1)
                        for r in range(3):
                            mm = pe.matmul(psF[:, n % 2, :], self.adjT[:, j, tile(t)], parts[:, j, r, :],
                                           start=(j == 0 and r == 0), stop=(j == NT - 1 and r == 2))
                    mm.then_inc(f_ready, 1)

                pe.wait_ge(ones_ready, 1)
                for t in range(NT):
                    for j in range(NT):
                        mm = pe.matmul(psD[:, t:t + 1], self.adjT[:, j, tile(t)], ones[:, 0:1],
                                       start=(j == 0 and t == 0), stop=(t == NT - 1 and j == NT - 1),
                                       skip_group_check=True)
                mm.then_inc(deg_ready, 1)
                for t in range(NT):
                    spread(0, t)
                pe.wait_ge(w_in, 16 * 2 * KD)
                pe.wait_ge(f_copied, NT)

                def weigh(t):
                    pe.wait_ge(f_copied, NT + t + 1)
                    for s in range(2):
                        if t >= 1:
                            pe.wait_ge(t_copied, 2 * t - 1 + s)
                        for k in range(KD):
                            src = F[:, t, tile(k)] if s == 0 else f2[:, t % 2, tile(k)]
                            mm = pe.transpose(psT[:, s, k, :], src, self.ident[:, :])
                        mm.then_inc(t_ready, 1)
                    if t >= 2:
                        pe.wait_ge(y_copied, t - 1)
                    for s in range(2):
                        pe.wait_ge(t_copied, 2 * t + s + 1)
                        for k in range(KD):
                            mm = pe.matmul(psY[:, t % 2, :], fT[:, s, k, :], w[:, s, k, :],
                                           start=(s == 0 and k == 0), stop=(s == 1 and k == KD - 1))
                    mm.then_inc(y_ready, 1)

                for t in range(NT):
                    spread(1, t)
                    if t >= 1:
                        weigh(t - 1)
                weigh(NT - 1)

    def transpose_stage(self, nat, tr):
        nc = self.nc
        with self.open() as st:
            psT = self.ps(st, "psT", [P, 2, KD, P])
            t_ready = self.sem(st, "t_ready")
            t_copied = self.sem(st, "t_copied")
            block = st.enter_context(nc.Block())

            @block.tensor
            def _(pe):
                for t in range(NT):
                    self.transpose_tiles(pe, psT, t, nat, t_ready, t_copied)

            @block.scalar
            def _(act):
                for t in range(NT):
                    act.wait_ge(t_ready, t + 1)
                    act.copy(tr[:, :, tile(t)], psT[:, t % 2, :, :]).then_inc(t_copied, 1)

    def top_p_step(self, nat, tr, new):
        nc, a = self.nc, self.a
        H = a["L1_gnn_W1"].shape[1]
        q, kk = slice(0, H), slice(H, 2 * H)
        with self.open() as st:
            QT = self.sb(st, "QT", [P, N])
            KT = self.sb(st, "KT", [P, N])
            with self.open() as s2:
                w13 = self.sb(s2, "w13", [P, KD, 2 * H])
                w2 = self.sb(s2, "w2", [H, H])
                psP = self.ps(s2, "psP", [P, 2, 512])
                psQ = self.ps(s2, "psQ", [P, 2, 512])
                w_in = self.sem(s2, "w_in")
                p_ready = self.sem(s2, "p_ready")
                p_copied = self.sem(s2, "p_copied")
                q_ready = self.sem(s2, "q_ready")
                q_copied = self.sem(s2, "q_copied")
                block = s2.enter_context(nc.Block())

                @block.sync
                def _(sp):
                    for n, name in enumerate(("L1_gnn_W1", "L1_gnn_W3")):
                        sp.dma_start(w13[:, :, n * H:(n + 1) * H],
                                     a[name].rearrange("(k p) h -> p k h", p=P)).then_inc(w_in, 16)
                    sp.dma_start(w2[:, :], a["L1_gnn_W2"]).then_inc(w_in, 16)

                @block.tensor
                def _(pe):
                    pe.wait_ge(w_in, 48)
                    for c in range(4):
                        if c >= 2:
                            pe.wait_ge(p_copied, c - 1)
                        for k in range(KD):
                            mm = pe.matmul(psP[:, c % 2, :], w13[:, k, :], tr[:, k, c * 512:(c + 1) * 512],
                                           start=(k == 0), stop=(k == KD - 1))
                        mm.then_inc(p_ready, 1)
                    for c in range(4):
                        pe.wait_ge(p_copied, c + 1)
                        if c >= 2:
                            pe.wait_ge(q_copied, c - 1)
                        pe.matmul(psQ[kk, c % 2, :], w2[:, :], KT[q, c * 512:(c + 1) * 512],
                                  start=True, stop=True).then_inc(q_ready, 1)

                @block.vector
                def _(dve):
                    for c in range(4):
                        dve.wait_ge(p_ready, c + 1)
                        dve.tensor_copy(KT[:, c * 512:(c + 1) * 512], psP[:, c % 2, :]).then_inc(p_copied, 1)

                @block.scalar
                def _(act):
                    for c in range(4):
                        act.wait_ge(q_ready, c + 1)
                        act.copy(QT[kk, c * 512:(c + 1) * 512], psQ[kk, c % 2, :]).then_inc(q_copied, 1)

            qs = self.sb(st, "qs", [P, P])
            below = self.sb(st, "below", [P, 2, N])
            expd = self.sb(st, "expd", [P, 2, N])
            junk = self.sb(st, "junk", [P, N], BF16)
            keptT = self.sb(st, "keptT", [P, NT, P])
            top = self.sb(st, "top", [P, 2])
            ntop = self.sb(st, "ntop", [P, 2])
            total = self.sb(st, "total", [P, 2])
            enough = self.sb(st, "enough", [P, 1])
            mass = self.sb(st, "mass", [P, 1])
            reach = self.sb(st, "reach", [P, 1])
            low = self.sb(st, "low", [P, 1])
            mid = self.sb(st, "mid", [P, 1])
            kept = self.sb(st, "kept", [P, 2])
            kinv = self.sb(st, "kinv", [P, 2])
            psL = self.ps(st, "psL", [P, N])
            psT = self.ps(st, "psT", [P, 2, 4, P])
            psO = self.ps(st, "psO", [P, D])
            qs_ready = self.sem(st, "qs_ready")
            logits_ready = self.sem(st, "logits_ready")
            ntop_ready = self.sem(st, "ntop_ready")
            below_ready = self.sem(st, "below_ready")
            exp_ready = self.sem(st, "exp_ready")
            kept_ready = self.sem(st, "kept_ready")
            t_ready = self.sem(st, "t_ready")
            t_copied = self.sem(st, "t_copied")
            o_ready = self.sem(st, "o_ready")
            o_copied = self.sem(st, "o_copied")
            dve_done = self.sem(st, "dve_done")
            block = st.enter_context(nc.Block())

            def wait(eng, sem, value):
                if not isinstance(value, int) or value > 0:
                    eng.wait_ge(sem, value)

            def sweep(eng, ahead, behind):
                ahead(0, 0)
                for t in range(2):
                    ahead(t + 1, (t + 1) % 2)
                    behind(t, t % 2)
                with eng.Fori(1, NT // 2 - 1) as pair:
                    for u in range(2):
                        ahead(pair * 2 + (u + 1), (u + 1) % 2)
                        behind(pair * 2 + u, u)
                ahead(NT - 1, 1)
                behind(NT - 2, 0)
                behind(NT - 1, 1)

            @block.tensor
            def _(pe):
                def logits(t, u):
                    pe.wait_ge(qs_ready, t + 1)
                    wait(pe, below_ready, t)
                    for c in range(4):
                        mm = pe.matmul(psL[:, c * 512:(c + 1) * 512], qs[kk, :], KT[kk, c * 512:(c + 1) * 512],
                                       start=True, stop=True)
                    mm.then_inc(logits_ready, 1)

                def apply(t, u):
                    pe.wait_ge(kept_ready, t + 1)
                    for gp in range(4):
                        if gp >= 2:
                            pe.wait_ge(t_copied, t * 4 + (gp - 1))
                        for j in range(4):
                            mm = pe.transpose(psT[:, gp % 2, j, :], expd[:, u, tile(4 * gp + j)], self.ident[:, :])
                        mm.then_inc(t_ready, 1)
                    wait(pe, o_copied, t)
                    for j in range(NT):
                        if j % 4 == 0:
                            pe.wait_ge(t_copied, t * 4 + (j // 4 + 1))
                        mm = pe.matmul(psO[:, :], keptT[:, j, :], nat[:, j, :], start=(j == 0), stop=(j == NT - 1))
                    mm.then_inc(o_ready, 1)

                sweep(pe, logits, apply)

            @block.scalar
            def _(act):
                def exps(t, u):
                    wait(act, logits_ready, t)
                    act.copy(qs[kk, :], QT[kk, bass.ds(t * P, P)]).then_inc(qs_ready, 1)
                    act.wait_ge(ntop_ready, t + 1)
                    wait(act, t_ready, t * 4 - 4)
                    act.activation(below[:, u, :], psL[:, :], ACT.Identity,
                                   bias=ntop[:, u:u + 1]).then_inc(below_ready, 1)
                    act.wait_ge(below_ready, t + 1)
                    act.activation(expd[:, u, :], below[:, u, :], ACT.Exp,
                                   accum_out=total[:, u:u + 1]).then_inc(exp_ready, 1)

                def copies(t, u):
                    for gp in range(4):
                        act.wait_ge(t_ready, t * 4 + (gp + 1))
                        wait(act, o_ready, t)
                        act.copy(keptT[:, 4 * gp:4 * gp + 4, :], psT[:, gp % 2, :, :]).then_inc(t_copied, 1)
                    act.wait_ge(o_ready, t + 1)
                    act.activation(new[:, bass.ds(t, 1), :].rearrange("p o d -> p (o d)"), psO[:, :], ACT.Copy,
                                   scale=kinv[:, u:u + 1]).then_inc(o_copied, 1)

                sweep(act, exps, copies)

            @block.vector
            def _(dve):
                n_done = [0, 0]
                PER_TILE = 1 + 1 + 4 * BISECTIONS + 1

                def at(t, offset):
                    n_done[0], n_done[1] = t * PER_TILE, offset

                def link(ins):
                    n_done[1] += 1
                    ins.then_inc(dve_done, 1)
                    dve.wait_ge(dve_done, n_done[0] + n_done[1])

                def tops(t, u):
                    dve.wait_ge(logits_ready, t + 1)
                    at(t, tops_offset(t))
                    link(dve.tensor_reduce(top[:, u:u + 1], psL[:, :], AX.X, ALU.max))
                    dve.tensor_scalar(ntop[:, u:u + 1], top[:, u:u + 1], -1.0, None, ALU.mult).then_inc(ntop_ready, 1)

                def tops_offset(t):
                    return 0 if isinstance(t, int) and t == 0 else -(PER_TILE - 1)

                def search(t, u):
                    at(t, 2 if not (isinstance(t, int) and t == NT - 1) else 1)
                    dve.wait_ge(exp_ready, t + 1)
                    dve.tensor_scalar(enough[:, :], total[:, u:u + 1], TOP_P, None, ALU.mult)
                    dve.memset(low[:, :], -16.0)
                    link(dve.memset(mid[:, :], -8.0))
                    for n in range(BISECTIONS):
                        step = 8.0 / 2 ** n
                        link(dve.scalar_tensor_tensor(junk[:, :], below[:, u, :], mid[:, 0:1], expd[:, u, :],
                                                      ALU.is_gt, ALU.mult, accum_out=mass[:, 0:1]))
                        link(dve.tensor_tensor(reach[:, :], mass[:, :], enough[:, :], ALU.is_ge))
                        link(dve.scalar_tensor_tensor(low[:, :], reach[:, :], step, low[:, :], ALU.mult, ALU.add))
                        link(dve.tensor_scalar(mid[:, :], low[:, :], step / 2, None, ALU.add))
                    link(dve.scalar_tensor_tensor(expd[:, u, :], below[:, u, :], low[:, 0:1], expd[:, u, :],
                                                  ALU.is_gt, ALU.mult, accum_out=kept[:, u:u + 1]))
                    dve.reciprocal(kinv[:, u:u + 1], kept[:, u:u + 1]).then_inc(kept_ready, 1)

                sweep(dve, tops, search)

    def mix_stage(self, nat, tr, u2_dram, y_dram, x_dram=None, x_new=None):
        nc, a = self.nc, self.a
        last = x_new is not None
        with self.open() as st:
            w = self.sb(st, "w", [P, KD, D])
            yt = self.sb(st, "yt", [P, 4, D])
            xt = self.sb(st, "xt", [P, 4, D])
            yo = self.sb(st, "yo", [P, 4, D])
            gam = self.sb(st, "gam", [P, D])
            bet = self.sb(st, "bet", [P, D])
            stats = self.sb(st, "stats", [P, 2, 6])
            mv = self.sb(st, "mv", [P, 2, 2])
            veps = self.sb(st, "veps", [P, 2])
            sd = self.sb(st, "sd", [P, 2])
            rstd = self.sb(st, "rstd", [P, 2])
            psT = self.ps(st, "psT", [P, 2, KD, P])
            psO = self.ps(st, "psO", [P, 2, D])
            w_in = self.sem(st, "w_in")
            y_in = [self.sem(st, f"y_in{i}") for i in range(4)]
            y_out = [self.sem(st, f"y_out{i}") for i in range(4)]
            t_ready = self.sem(st, "t_ready")
            t_copied = self.sem(st, "t_copied")
            o_ready = self.sem(st, "o_ready")
            o_read = self.sem(st, "o_read")
            y_ready = self.sem(st, "y_ready")
            v_ready = self.sem(st, "v_ready")
            sd_ready = self.sem(st, "sd_ready")
            dve_done = self.sem(st, "dve_done")
            block = st.enter_context(nc.Block())
            n_in = 32 if last else 16

            @block.sync
            def _(sp):
                for k in range(KD):
                    sp.dma_start(w[:, k, :], u2_dram[tile(k), :]).then_inc(w_in, 16)
                if last:
                    sp.dma_start(gam[:, :], a["L1_gnn_gamma"].partition_broadcast(P)).then_inc(w_in, 16)
                    sp.dma_start(bet[:, :], a["L1_gnn_beta"].partition_broadcast(P)).then_inc(w_in, 16)
                for t in range(NT):
                    if t >= 4:
                        sp.wait_ge(y_ready, t - 3)
                    sp.dma_start(yt[:, t % 4, :], y_dram[tile(t), :]).then_inc(y_in[t % 4], 16)
                    if last:
                        sp.dma_start(xt[:, t % 4, :], x_dram[tile(t), :]).then_inc(y_in[t % 4], 16)

            @block.gpsimd
            def _(pool):
                for t in range(NT):
                    pool.wait_ge(y_ready, t + 1)
                    pool.dma_start((x_new if last else y_dram)[tile(t), :], yo[:, t % 4, :]).then_inc(y_out[t % 4], 16)
                for i in range(4):
                    pool.wait_ge(y_out[i], 16 * (NT // 4))

            @block.tensor
            def _(pe):
                for t in range(NT):
                    self.transpose_tiles(pe, psT, t, nat, t_ready, t_copied)
                pe.wait_ge(w_in, 16 * (KD + (2 if last else 0)))
                for t in range(NT):
                    pe.wait_ge(t_copied, t + 1)
                    if t >= 2:
                        pe.wait_ge(o_read, t - 1)
                    for k in range(KD):
                        mm = pe.matmul(psO[:, t % 2, :], tr[:, k, tile(t)], w[:, k, :],
                                       start=(k == 0), stop=(k == KD - 1))
                    mm.then_inc(o_ready, 1)

            @block.scalar
            def _(act):
                for t in range(NT):
                    act.wait_ge(t_ready, t + 1)
                    act.copy(tr[:, :, tile(t)], psT[:, t % 2, :, :]).then_inc(t_copied, 1)
                if last:
                    for t in range(NT):
                        act.wait_ge(v_ready, t + 1)
                        act.activation(sd[:, t % 2:t % 2 + 1], veps[:, t % 2:t % 2 + 1], ACT.Sqrt).then_inc(sd_ready, 1)

            @block.vector
            def _(dve):
                link = chain(dve, dve_done)
                dve.wait_ge(w_in, 16 * (KD + (2 if last else 0)))
                for t in range(NT):
                    u, v = t % 4, t % 2
                    dve.wait_ge(o_ready, t + 1)
                    dve.wait_ge(y_in[u], n_in * (t // 4 + 1))
                    if t >= 4:
                        dve.wait_ge(y_out[u], 16 * (t // 4))
                    ins = dve.tensor_tensor(yo[:, u, :], psO[:, v, :], yt[:, u, :], ALU.add)
                    ins.then_inc(o_read, 1)
                    dve.wait_ge(o_read, t + 1)
                    if last:
                        link(dve.bn_stats(stats[:, v, :], yo[:, u, :]))
                        link(dve.bn_aggr(mv[:, v, :], stats[:, v, :]))
                        dve.tensor_scalar(veps[:, v:v + 1], mv[:, v, 1:2], LN_EPS, None, ALU.add).then_inc(v_ready, 1)
                        dve.wait_ge(sd_ready, t + 1)
                        link(dve.reciprocal(rstd[:, v:v + 1], sd[:, v:v + 1]))
                        link(dve.tensor_scalar(yo[:, u, :], yo[:, u, :], mv[:, v, 0:1], rstd[:, v:v + 1],
                                               ALU.subtract, ALU.mult))
                        link(dve.tensor_tensor(yo[:, u, :], yo[:, u, :], gam[:, :], ALU.mult))
                        link(dve.tensor_tensor(yo[:, u, :], yo[:, u, :], bet[:, :], ALU.add))
                        dve.tensor_tensor(yo[:, u, :], yo[:, u, :], xt[:, u, :], ALU.add).then_inc(y_ready, 1)
                    else:
                        dve.tensor_scalar(yo[:, u, 0:1], yo[:, u, 0:1], 1.0, None, ALU.mult).then_inc(y_ready, 1)

    def top_p_stage(self, natA, trA, natB, trB, x_dram, x_new, y_dram):
        self.transpose_stage(natA, trB)
        self.top_p_step(natA, trB, natB)
        self.mix_stage(natB, trA, self.a["L1_gnn_U2_0"], y_dram)
        self.top_p_step(natB, trA, natA)
        self.mix_stage(natA, trB, self.a["L1_gnn_U2_1"], y_dram, x_dram, x_new)

    def relation_table(self, pool, st, table):
        pairs_dram = self.a["L3_gnn_rel_pair_index"]
        E = pairs_dram.shape[0]
        R = next(r for r in range(P, 0, -1) if E % r == 0)
        C = E // R
        zeros, pairs, index, ones = self.rel_bufs
        ready = self.rel_sems["ready"]
        pool.dma_start(pairs[0:R, :, :], pairs_dram.rearrange("(r c) o -> r c o", r=R)).then_inc(self.rel_sems["in"], 16)
        pool.memset(ones[:, :], 1.0).then_inc(ready, 1)
        pool.memset(zeros[:, :], 0.0).then_inc(ready, 1)
        pool.wait_ge(ready, 2)
        width = zeros.shape[1]
        rows = table.rearrange("(b p w) o -> b p (w o)", p=P, w=width)
        for b in range(rows.shape[0]):
            pool.dma_start(rows[b], zeros[:, :]).then_inc(self.rel_sems["cleared"], 16)
        pool.wait_ge(self.rel_sems["in"], 16)
        pool.tensor_scalar(pairs[0:R, :, 0], pairs[0:R, :, 0], float(N), None, ALU.mult).then_inc(ready, 1)
        pool.wait_ge(ready, 3)
        pool.tensor_tensor(index[0:R, :], pairs[0:R, :, 0], pairs[0:R, :, 1], ALU.add).then_inc(ready, 1)
        pool.wait_ge(ready, 4)
        pool.wait_ge(self.rel_sems["cleared"], 16 * rows.shape[0])
        for c in range(C):
            pool.indirect_dma_start(out=table, out_offset=bass.IndirectOffsetOnAxis(ap=index[0:R, c:c + 1], axis=0),
                                    in_=ones[0:R, :], in_offset=None).then_inc(self.rel_sems["marked"], 16)
            pool.wait_ge(self.rel_sems["marked"], 16 * (c + 1))

    def relation_project_stage(self, tr, KT, qT_dram):
        nc, a = self.nc, self.a
        scale = (D // self.REL_HEADS) ** -0.5
        with self.open() as st:
            wq = self.sb(st, "wq", [P, KD, D])
            wk = self.sb(st, "wk", [P, KD, D])
            self.weight_transpose_stage([(a["L3_gnn_Wq"], wq), (a["L3_gnn_Wk"], wk)])
            bias = self.sb(st, "bias", [P, 2, KD])
            biasq = self.sb(st, "biasq", [P, KD])
            QT = self.sb(st, "QT", [P, KD, N])
            psL = self.ps(st, "psL", [P, 2, 512])
            b_in = self.sem(st, "b_in")
            bq_ready = self.sem(st, "bq_ready")
            l_ready = self.sem(st, "l_ready")
            l_done = self.sem(st, "l_done")
            q_out = self.sem(st, "q_out")
            block = st.enter_context(nc.Block())
            steps = [(i, m, c) for i in range(2) for m in range(KD) for c in range(N // 512)]

            @block.sync
            def _(sp):
                for i, name in enumerate(("L3_gnn_bq", "L3_gnn_bk")):
                    sp.dma_start(bias[:, i, :], a[name].rearrange("(m p) -> p m", p=P),
                                 allow_slow_non_contiguous=True).then_inc(b_in, 16)
                for m in range(KD):
                    sp.wait_ge(l_done, 4 * (m + 1))
                    sp.dma_start(qT_dram[m], QT[:, m, :]).then_inc(q_out, 16)
                sp.wait_ge(q_out, 16 * KD)

            @block.vector
            def _(dve):
                dve.wait_ge(b_in, 32)
                dve.tensor_scalar(biasq[:, :], bias[:, 0, :], scale, None, ALU.mult).then_inc(bq_ready, 1)

            @block.scalar
            def _(act):
                act.wait_ge(bq_ready, 1)
                for n, (i, m, c) in enumerate(steps):
                    act.wait_ge(l_ready, n + 1)
                    dst, b = (QT, biasq[:, m:m + 1]) if i == 0 else (KT, bias[:, 1, m:m + 1])
                    act.activation(dst[:, m, c * 512:(c + 1) * 512], psL[:, n % 2, :], ACT.Identity, bias=b,
                                   scale=scale if i == 0 else 1.0).then_inc(l_done, 1)

            @block.tensor
            def _(pe):
                for n, (i, m, c) in enumerate(steps):
                    if n >= 2:
                        pe.wait_ge(l_done, n - 1)
                    for k in range(KD):
                        mm = pe.matmul(psL[:, n % 2, :], (wq, wk)[i][:, k, tile(m)], tr[:, k, c * 512:(c + 1) * 512],
                                       start=(k == 0), stop=(k == KD - 1))
                    mm.then_inc(l_ready, 1)

    def relation_stage(self, nat, Bflat, KT, qT_dram, table, x_dram, out):
        nc, a, H = self.nc, self.a, self.REL_HEADS
        DK = D // H
        HALF = N // 2
        with self.open() as st:
            Gb = self.sb(st, "Gb", [P, H // 2, N])
            Ga = Bflat[:, :].rearrange("p (h n) -> p h n", h=H // 2)
            G = [Ga[:, h, :] if h < H // 2 else Gb[:, h - H // 2, :] for h in range(H)]
            edge = self.sb(st, "edge", [P, N])
            rel = self.sb(st, "rel", [P, N])
            plain = self.sb(st, "plain", [P, N], BF16)
            veil = self.sb(st, "veil", [P, N], BF16)
            attn = self.sb(st, "attn", [P, N])
            attnT = self.sb(st, "attnT", [P, NT, P])
            ramp = self.sb(st, "ramp", [P, N], mybir.dt.int16)
            tbase = self.sb(st, "tbase", [P, NT])
            std = self.sb(st, "std", [P, 1])
            qs = self.sb(st, "qs", [P, KD, P])
            xt = self.sb(st, "xt", [P, D])
            xo = self.sb(st, "xo", [P, D])
            y = self.sb(st, "y", [P, D])
            m0 = self.sb(st, "m0", [P, H])
            m1 = self.sb(st, "m1", [P, H])
            nm = self.sb(st, "nm", [P, H])
            pad = self.sb(st, "pad", [P, 2 * H])
            zr = self.sb(st, "zr", [P, H])
            e0 = self.sb(st, "e0", [P, H])
            ed = self.sb(st, "ed", [P, H])
            z = self.sb(st, "z", [P, H])
            rz = self.sb(st, "rz", [P, H])
            w0 = self.sb(st, "w0", [P, H])
            wd = self.sb(st, "wd", [P, H])
            nplain = self.sb(st, "nplain", [P, 1])
            om = self.sb(st, "om", [P, 1])
            own = self.sb(st, "own", [P, 2])
            psS = self.ps(st, "psS", [P, 2, HALF])
            psT = self.ps(st, "psT", [P, 2, 4, P])
            psO = self.ps(st, "psO", [P, D])
            const_ready = self.sem(st, "const_ready")
            rows_in = self.sem(st, "rows_in")
            q_in = self.sem(st, "q_in")
            x_in = self.sem(st, "x_in")
            x_out = self.sem(st, "x_out")
            masks_made = self.sem(st, "masks_made")
            scores_ready = self.sem(st, "scores_ready")
            scores_read = self.sem(st, "scores_read")
            nm_ready = self.sem(st, "nm_ready")
            exps_ready = self.sem(st, "exps_ready")
            attn_ready = self.sem(st, "attn_ready")
            t_ready = self.sem(st, "t_ready")
            t_copied = self.sem(st, "t_copied")
            o_ready = self.sem(st, "o_ready")
            xo_ready = self.sem(st, "xo_ready")
            dve_done = self.sem(st, "dve_done")
            block = st.enter_context(nc.Block())

            def wait(eng, sem, value):
                if not isinstance(value, int) or value > 0:
                    eng.wait_ge(sem, value)

            def sweep(eng, body, rest=None):
                body(0)
                body(1, lambda: rest(0)) if rest else body(1)
                with eng.Fori(2, NT) as t:
                    if rest:
                        body(t, lambda: rest(t - 1))
                    else:
                        body(t)
                if rest:
                    rest(NT - 1)

            @block.gpsimd
            def _(pool):
                pool.iota(ramp[:, :], pattern=[[1, N]], base=0, channel_multiplier=-1).then_inc(const_ready, 1)
                pool.memset(std[:, :], REL_STD).then_inc(const_ready, 1)
                for t in range(NT):
                    pool.memset(tbase[:, t:t + 1], float(t * P)).then_inc(const_ready, 1)
                def body(t):
                    pool.wait_ge(xo_ready, t + 1)
                    pool.dma_start(out[bass.ds(t * P, P), :], xo[:, :]).then_inc(x_out, 16)
                sweep(pool, body)
                pool.wait_ge(x_out, 16 * NT)

            @block.sync
            def _(sp):
                for t in range(NT):
                    wait(sp, masks_made, t)
                    sp.dma_start(edge[:, :], a["adj"][bass.ds(t * P, P), :]).then_inc(rows_in, 16)
                    sp.dma_start(rel[:, :], table.rearrange("(i j) o -> i (j o)", j=N)[bass.ds(t * P, P), :]
                                 ).then_inc(rows_in, 16)
                    wait(sp, scores_ready, t * 2 * H)
                    sp.dma_start(qs[:, :, :], qT_dram[:, :, bass.ds(t * P, P)].rearrange("m p i -> p m i")
                                 ).then_inc(q_in, 16)
                    wait(sp, xo_ready, t)
                    sp.dma_start(xt[:, :], x_dram[bass.ds(t * P, P), :]).then_inc(x_in, 16)

            @block.tensor
            def _(pe):
                def apply(t):
                    pe.wait_ge(attn_ready, t + 1)
                    for gp in range(4):
                        if gp >= 2:
                            pe.wait_ge(t_copied, t * 4 + (gp - 1))
                        for j in range(4):
                            mm = pe.transpose(psT[:, gp % 2, j, :], attn[:, tile(4 * gp + j)], self.ident[:, :])
                        mm.then_inc(t_ready, 1)
                    wait(pe, xo_ready, t)
                    for j in range(NT):
                        if j % 4 == 0:
                            pe.wait_ge(t_copied, t * 4 + (j // 4 + 1))
                        mm = pe.matmul(psO[:, :], attnT[:, j, :], nat[:, j, :], start=(j == 0), stop=(j == NT - 1))
                    mm.then_inc(o_ready, 1)

                def body(t, rest=None):
                    pe.wait_ge(q_in, t * 16 + 16)
                    for h in range(H):
                        r = slice((h * DK) % P, (h * DK) % P + DK)
                        m = h * DK // P
                        for half in range(2):
                            n = 2 * h + half
                            wait(pe, scores_read, t * 2 * H + (n - 1))
                            for c in range(2):
                                o = half * HALF + c * 512
                                mm = pe.matmul(psS[:, half, c * 512:(c + 1) * 512], qs[r, m, :], KT[r, m, o:o + 512],
                                               start=True, stop=True)
                            mm.then_inc(scores_ready, 1)
                    if rest:
                        rest()
                sweep(pe, body, apply)

            @block.scalar
            def _(act):
                act.wait_ge(const_ready, 2)

                def copies(t):
                    for gp in range(4):
                        act.wait_ge(t_ready, t * 4 + (gp + 1))
                        wait(act, o_ready, t)
                        act.copy(attnT[:, 4 * gp:4 * gp + 4, :], psT[:, gp % 2, :, :]).then_inc(t_copied, 1)

                def body(t, rest=None):
                    for h in range(H):
                        act.wait_ge(nm_ready, t * H + (h + 1))
                        act.activation(G[h], G[h], ACT.Exp, bias=nm[:, h:h + 1], accum_out=zr[:, h:h + 1])
                    act.activation(e0[:, :], nm[:, :], ACT.Exp)
                    act.activation(ed[:, :], nm[:, :], ACT.Exp, bias=std[:, 0:1]).then_inc(exps_ready, 1)
                    if rest:
                        rest()
                sweep(act, body, copies)

            @block.vector
            def _(dve):
                FIRST = 2 + 6 + 3 * H
                base = [0, 0]

                def link(ins):
                    base[1] += 1
                    ins.then_inc(dve_done, 1)
                    dve.wait_ge(dve_done, base[0] + base[1])

                dve.wait_ge(const_ready, 2 + NT)

                def finish(t):
                    dve.wait_ge(o_ready, t + 1)
                    dve.wait_ge(x_in, t * 16 + 16)
                    link(dve.scalar_tensor_tensor(y[:, :], nat[:, bass.ds(t, 1), :].rearrange("p o d -> p (o d)"),
                                                  own[:, 1:2], psO[:, :], ALU.mult, ALU.add))
                    wait(dve, x_out, t * 16)
                    dve.tensor_tensor(xo[:, :], y[:, :], xt[:, :], ALU.add).then_inc(xo_ready, 1)

                def body(t, rest=None):
                    base[0], base[1] = (0, 0) if rest is None else (t * (FIRST + 2) - 2, 0)
                    dve.wait_ge(rows_in, t * 32 + 32)
                    link(dve.scalar_tensor_tensor(edge[:, :], ramp[:, :], tbase[:, bass.ds(t, 1)], edge[:, :],
                                                  ALU.not_equal, ALU.mult))
                    link(dve.tensor_tensor(rel[:, :], edge[:, :], rel[:, :], ALU.mult))
                    dve.tensor_scalar(veil[:, :], rel[:, :], -1.0, BIG, ALU.add, ALU.mult)
                    ins = dve.scalar_tensor_tensor(plain[:, :], edge[:, :], 1.0, rel[:, :], ALU.mult, ALU.subtract,
                                                   accum_out=nplain[:, 0:1])
                    ins.then_inc(masks_made, 1)
                    dve.wait_ge(masks_made, t + 1)
                    for h in range(H):
                        for half in range(2):
                            n = 2 * h + half
                            cols = slice(half * HALF, (half + 1) * HALF)
                            dve.wait_ge(scores_ready, t * 2 * H + (n + 1))
                            base[1] += 1
                            dve.memset(pad[:, n:n + 1], 0.0).then_inc(dve_done, 1)
                            dve.tensor_tensor_reduce(
                                G[h][:, cols], psS[:, half, :], veil[:, cols], 1.0,
                                REL_STD if half == 0 else m0[:, h:h + 1], ALU.add, ALU.max,
                                (m0 if half == 0 else m1)[:, h:h + 1]).then_inc(scores_read, 1)
                            dve.wait_ge(scores_read, t * 2 * H + (n + 1))
                        dve.tensor_scalar(nm[:, h:h + 1], m1[:, h:h + 1], -1.0, None, ALU.mult).then_inc(nm_ready, 1)
                    dve.wait_ge(exps_ready, t + 1)
                    link(dve.scalar_tensor_tensor(z[:, :], e0[:, :], nplain[:, 0:1], zr[:, :], ALU.mult, ALU.add))
                    link(dve.tensor_tensor(z[:, :], z[:, :], ed[:, :], ALU.add))
                    link(dve.reciprocal(rz[:, :], z[:, :]))
                    link(dve.tensor_scalar(rz[:, :], rz[:, :], 1.0 / H, None, ALU.mult))
                    dve.tensor_tensor(w0[:, :], e0[:, :], rz[:, :], ALU.mult)
                    link(dve.tensor_tensor(wd[:, :], ed[:, :], rz[:, :], ALU.mult))
                    if rest:
                        link(dve.tensor_copy(own[:, 1:2], own[:, 0:1]))
                    dve.tensor_reduce(om[:, :], w0[:, :], AX.X, ALU.add)
                    link(dve.tensor_reduce(own[:, 0:1], wd[:, :], AX.X, ALU.add))
                    wait(dve, t_ready, t * 4)
                    for h in range(H):
                        if h == 0:
                            link(dve.tensor_scalar(attn[:, :], G[0], rz[:, 0:1], None, ALU.mult))
                        else:
                            link(dve.scalar_tensor_tensor(attn[:, :], G[h], rz[:, h:h + 1], attn[:, :],
                                                          ALU.mult, ALU.add))
                    dve.scalar_tensor_tensor(attn[:, :], plain[:, :], om[:, 0:1], attn[:, :],
                                             ALU.mult, ALU.add).then_inc(attn_ready, 1)
                    dve.wait_ge(attn_ready, t + 1)
                    if rest:
                        rest()
                    return base[1]

                assert body(0) == FIRST
                assert body(1, lambda: finish(0)) == FIRST + 2
                with dve.Fori(2, NT) as t:
                    assert body(t, lambda: finish(t - 1)) == FIRST + 2
                base[0], base[1] = NT * (FIRST + 2) - 2, 0
                link(dve.tensor_copy(own[:, 1:2], own[:, 0:1]))
                finish(NT - 1)


class Factors:
    def __init__(self, b, st, H, sT_dram, top_dram):
        self.thr, self.steep, self.colE, self.colF, self.rowE, self.rowF = (
            b.sb(st, name, [P, H, NT]) for name in ("thr", "steep", "colE", "colF", "rowE", "rowF"))
        self.sT_dram, self.top_dram = sT_dram, top_dram


def program(nc, a, out):
    b = Build(nc, a, out)
    xa = nc.dram_tensor("xa", [N, D], F32).ap()
    xb = nc.dram_tensor("xb", [N, D], F32).ap()
    xc = nc.dram_tensor("xc", [N, D], F32).ap()
    y_dram = nc.dram_tensor("y_dram", [N, D], F32).ap()
    qT_dram = nc.dram_tensor("qT_dram", [KD, P, N], F32).ap()
    b.table = nc.dram_tensor("rel_table", [N * N, 1], F32).ap()
    sT_dram = nc.dram_tensor("sT_dram", [32, N], F32).ap()
    top_dram = nc.dram_tensor("top_dram", [32], F32).ap()
    with b.open() as st:
        b.ident = b.sb(st, "ident", [P, P])
        A = b.sb(st, "A", [P, NT * D])
        B = b.sb(st, "B", [P, NT * D])
        natA, natB = (v[:, :].rearrange("p (t d) -> p t d", t=NT) for v in (A, B))
        trA, trB = (v[:, :].rearrange("p (k n) -> p k n", k=KD) for v in (A, B))
        with b.open() as st_adj:
            b.adjT = b.sb(st_adj, "adjT", [P, NT, N], BF16)
            b.adjacency_stage()
            b.norm_stage(a["x"], natA, trB)
            with b.open() as sg:
                g = Factors(b, sg, 16, sT_dram, top_dram)
                b.project_stage(16, 32, a["L0_gnn_W_seq"], a["L0_gnn_a1"], a["L0_gnn_a2"], natA, trB, g)
                b.attention_stage(16, 32, 8, [1, 2, 3, 5, 6, 7, 9, 10, 11, 13, 14, 15], natA, natB, g)
            b.elu_out_stage(natB, trA, a["L0_gnn_W_out"], a["L0_gnn_b_out"], a["x"], xa)
            b.diffusion_stage(natA, trA, natB, xa, y_dram)
            b.top_p_stage(natA, trA, natB, trB, xa, xb, y_dram)
            b.norm_stage(xb, natA, trB)
            with b.open() as sg:
                g = Factors(b, sg, 8, sT_dram, top_dram)
                b.project_stage(8, 64, a["L2_gnn_W"], a["L2_gnn_a1"], a["L2_gnn_a2"], natA, trB, g)
                b.attention_stage(8, 64, 4, [3, 7, 11, 15], natA, natB, g)
            b.mlp_stage(natB, trA, xb, xc)
        b.norm_stage(xc, natA, trB)
        with b.open() as sk:
            KT = b.sb(sk, "KT3", [P, KD, N])
            b.relation_project_stage(trB, KT, qT_dram)
            b.relation_stage(natA, B, KT, qT_dram, b.table, xc, out)


_INS = ["x", "adj", "L0_gnn_W_seq", "L0_gnn_a1", "L0_gnn_a2", "L0_gnn_W_out", "L0_gnn_b_out",
        "L1_gnn_W1", "L1_gnn_W2", "L1_gnn_W3", "L1_gnn_U1_0", "L1_gnn_U1_1", "L1_gnn_U2_0", "L1_gnn_U2_1",
        "L1_gnn_gamma", "L1_gnn_beta", "L2_gnn_W", "L2_gnn_a1", "L2_gnn_a2", "L2_gnn_W1", "L2_gnn_b1",
        "L2_gnn_W2", "L2_gnn_b2", "L2_gnn_W3", "L2_gnn_b3", "L2_gnn_W4", "L2_gnn_b4",
        "L3_gnn_rel_pair_index", "L3_gnn_Wq", "L3_gnn_bq", "L3_gnn_Wk", "L3_gnn_bk"]


def kernel(**inputs):
    import numpy as _np
    import concourse.bacc as _bacc
    from concourse import mybir as _mybir
    from concourse.bass_utils import run_bass_kernel_spmd as _run

    nc = _bacc.Bacc("TRN2", target_bir_lowering=False, num_devices=1)
    arrays, aps = {}, {}
    for name in _INS:
        array = _np.ascontiguousarray(inputs[name])
        arrays[f"in_{name}_dram"] = array
        aps[name] = nc.dram_tensor(f"in_{name}_dram", array.shape, _mybir.dt.from_np(array.dtype),
                                   kind="ExternalInput").ap()
    out = nc.dram_tensor("out_0_dram", (N, D), _mybir.dt.float32, kind="ExternalOutput").ap()
    program(nc, aps, out)
    r = _run(nc, [arrays], core_ids=[0])
    return r.results[0]["out_0_dram"]
```
